# Optimizing a Trainium2 kernel written in Bass

```python
import numpy as np
import jax
import jax.numpy as jnp

def _softmax(x, axis=-1):
    return jax.nn.softmax(x, axis=axis)

def _gelu(x):
    return jax.nn.gelu(x, approximate=True)

def _silu(x):
    return jax.nn.silu(x)

def _sigmoid(x):
    return jax.nn.sigmoid(x)

def _layernorm(x, axis=-1, eps=1e-05):
    m = jnp.mean(x, axis=axis, keepdims=True)
    v = jnp.var(x, axis=axis, keepdims=True)
    return (x - m) / jnp.sqrt(v + eps)

def _scatter_add(tgt, idx, src, axis=0):
    return tgt.at[idx].add(src)

def _segment_sum(src, seg, n):
    return jax.ops.segment_sum(src, seg, n)
kernel_name = 'mk_flamingo_gated_d1_seqx_r4_ff72a6'

def setup_inputs(seed: int=0):
    np.random.seed(seed)
    _w = jnp.asarray

    def _rec_inputs():
        import jax
        import jax.numpy as jnp
        _rk = jax.random.key(seed)
        x = 7.22e-05 + 1 * jax.random.normal(jax.random.fold_in(_rk, 1), (4, 512, 512), jnp.float32)
        _lenS = 512 - jax.random.randint(jax.random.fold_in(_rk, 7), (4,), 0, max(1, 512 // 4) + 1, jnp.int32)
        _lenS2 = 512 - jax.random.randint(jax.random.fold_in(_rk, 8), (4,), 0, max(1, 512 // 4) + 1, jnp.int32)
        _ctx_1024P = jax.random.normal(jax.random.fold_in(_rk, 11), (4, 16, 256), jnp.float32)
        _ctx_1024c = jax.random.dirichlet(jax.random.fold_in(_rk, 511), 0.3 * jnp.ones((16,), jnp.float32), (4, 512))
        _ctx_1024t = jnp.einsum('bsk,bkd->bsd', _ctx_1024c, _ctx_1024P)
        _ctx_1024t = _ctx_1024t * jax.lax.rsqrt(jnp.mean(jnp.square(_ctx_1024t)) + 1e-12) * 0.953939
        ctx_1024 = 2.81802e-05 + 1.00001 * (_ctx_1024t + 0.3 * jax.random.normal(jax.random.fold_in(_rk, 611), (4, 512, 256), jnp.float32))
        _g = jax.random.normal(jax.random.fold_in(_rk, 9001), (2, 1), jnp.float32)
        _g = jnp.sign(_g) * jnp.maximum(jnp.abs(_g), 1.0) + (_g == 0) * 1.0
        g_xattn = _g[0]
        g_ffn = _g[1]
        return (x, ctx_1024, g_xattn, g_ffn)
    x, ctx_1024, g_xattn, g_ffn = _rec_inputs()

    def _L0_xattn_setup():
        import jax, jax.numpy as jnp
        import numpy as np
        key = jax.random.key(seed)
        ks = jax.random.split(key, 6)
        B, L, N, C, D = (8, 128, 512, 256, 128)
        return {'teacher_logits': jax.random.normal(ks[0], (B, L, N), dtype=jnp.float32), 'teacher_features': jax.random.normal(ks[1], (B, N, C), dtype=jnp.float32), 'Wq': jax.random.normal(ks[2], (D, C), dtype=jnp.float32) * (1.0 / np.sqrt(C)), 'bq': jnp.zeros((D,), dtype=jnp.float32), 'Wk': jax.random.normal(ks[3], (D, C), dtype=jnp.float32) * (1.0 / np.sqrt(C)), 'bk': jnp.zeros((D,), dtype=jnp.float32)}
    _L0_xattn_all = _L0_xattn_setup()
    _L0_xattn_in = {k: v for k, v in _L0_xattn_all.items() if k in ('Wq', 'bq', 'Wk', 'bk')}
    del _L0_xattn_all

    def _L0_ffn_setup():
        import jax, jax.numpy as jnp
        import numpy as np
        E = 8
        K = 2
        DIM = 512
        INTER = 352
        N_SHARED = 2
        STD = 0.02
        key = jax.random.key(seed)
        ks = jax.random.split(key, 9)
        B, S = (2, 512)
        return {'x': jax.random.normal(ks[0], (B, S, DIM), dtype=jnp.float32), 'gate_w': jax.random.normal(ks[1], (E, DIM), dtype=jnp.float32) * STD, 'router_bias': jnp.zeros((E,), dtype=jnp.float32), 'W1': jax.random.normal(ks[2], (E, DIM, INTER), dtype=jnp.float32) * STD, 'W3': jax.random.normal(ks[3], (E, DIM, INTER), dtype=jnp.float32) * STD, 'W2': jax.random.normal(ks[4], (E, INTER, DIM), dtype=jnp.float32) * STD, 'sw1': jax.random.normal(ks[5], (N_SHARED * INTER, DIM), dtype=jnp.float32) * STD, 'sw3': jax.random.normal(ks[6], (N_SHARED * INTER, DIM), dtype=jnp.float32) * STD, 'sw2': jax.random.normal(ks[7], (DIM, N_SHARED * INTER), dtype=jnp.float32) * STD}
    _L0_ffn_all = _L0_ffn_setup()
    _L0_ffn_in = {k: v for k, v in _L0_ffn_all.items() if k in ('gate_w', 'router_bias', 'W1', 'W3', 'W2', 'sw1', 'sw3', 'sw2')}
    del _L0_ffn_all
    return {'x': x, 'ctx_1024': ctx_1024, 'g_xattn': g_xattn, 'g_ffn': g_ffn, 'L0_xattn_Wq': _L0_xattn_in['Wq'], 'L0_xattn_bq': _L0_xattn_in['bq'], 'L0_xattn_Wk': _L0_xattn_in['Wk'], 'L0_xattn_bk': _L0_xattn_in['bk'], 'L0_ffn_gate_w': _L0_ffn_in['gate_w'], 'L0_ffn_router_bias': _L0_ffn_in['router_bias'], 'L0_ffn_W1': _L0_ffn_in['W1'], 'L0_ffn_W3': _L0_ffn_in['W3'], 'L0_ffn_W2': _L0_ffn_in['W2'], 'L0_ffn_sw1': _L0_ffn_in['sw1'], 'L0_ffn_sw3': _L0_ffn_in['sw3'], 'L0_ffn_sw2': _L0_ffn_in['sw2']}

def reference(x, ctx_1024, g_xattn, g_ffn, L0_xattn_Wq, L0_xattn_bq, L0_xattn_Wk, L0_xattn_bk, L0_ffn_gate_w, L0_ffn_router_bias, L0_ffn_W1, L0_ffn_W3, L0_ffn_W2, L0_ffn_sw1, L0_ffn_sw3, L0_ffn_sw2):
    import jax
    import jax.numpy as jnp

    def _L0_xattn_ref(teacher_logits, teacher_features, Wq, bq, Wk, bk):
        import jax, jax.numpy as jnp
        import numpy as np
        query = jnp.einsum('bnc,dc->bnd', teacher_features, Wq) + bq
        key = jnp.einsum('bnc,dc->bnd', teacher_features, Wk) + bk
        energy = jnp.einsum('bnd,bmd->bnm', query, key)
        attention = jax.nn.softmax(energy, axis=-1)
        x_m = jnp.einsum('bln,bmn->blm', teacher_logits, attention)
        return x_m

    def _L0_ffn_ref(x, gate_w, router_bias, W1, W3, W2, sw1, sw3, sw2):
        import jax, jax.numpy as jnp
        import numpy as np
        E = 8
        K = 2
        DIM = 512
        INTER = 352
        N_SHARED = 2
        STD = 0.02
        B, S, D = x.shape
        X = x.reshape(-1, D)
        T = X.shape[0]
        logits = jnp.einsum('td,ed->te', X, gate_w)
        scores = jax.nn.sigmoid(logits)
        sel = scores + router_bias[None, :]
        _, idx = jax.lax.top_k(sel, K)
        w = jnp.take_along_axis(scores, idx, axis=1)
        w = w / jnp.clip(jnp.sum(w, axis=-1, keepdims=True), 1e-12)
        gate_full = jnp.zeros((T, E), dtype=w.dtype).at[jnp.arange(T)[:, None], idx].set(w)
        h1 = jnp.einsum('td,edh->eth', X, W1)
        h3 = jnp.einsum('td,edh->eth', X, W3)
        y = jnp.einsum('eth,ehd->etd', jax.nn.silu(h1) * h3, W2)
        out = jnp.einsum('etd,te->td', y, gate_full)
        shared = jnp.einsum('th,dh->td', jax.nn.silu(jnp.einsum('td,hd->th', X, sw1)) * jnp.einsum('td,hd->th', X, sw3), sw2)
        out = out + shared
        return out.reshape(B, S, D)
    x = x + jnp.tanh(g_xattn[0]) * _L0_xattn_ref(_layernorm(x, axis=-1), ctx_1024, L0_xattn_Wq, L0_xattn_bq, L0_xattn_Wk, L0_xattn_bk)
    x = x + jnp.tanh(g_ffn[0]) * _L0_ffn_ref(_layernorm(x, axis=-1), L0_ffn_gate_w, L0_ffn_router_bias, L0_ffn_W1, L0_ffn_W3, L0_ffn_W2, L0_ffn_sw1, L0_ffn_sw3, L0_ffn_sw2)
    return x

_drawn_inputs = setup_inputs


def setup_inputs(seed=0):
    import zlib

    import numpy as np

    out = dict(_drawn_inputs(seed))
    spreads = {'L0_xattn_bq': (0.0, 0.1), 'L0_xattn_bk': (0.0, 0.1), 'L0_ffn_router_bias': (0.0, 0.1)}
    factors = {}
    for name, (base, spread) in spreads.items():
        noise = np.random.default_rng([zlib.crc32(name.encode()), seed]).standard_normal(out[name].shape)
        drawn = base * np.exp(spread * noise) if base else spread * noise
        out[name] = jnp.asarray(drawn.astype(out[name].dtype))
    for name, factor in factors.items():
        out[name] = (out[name] * factor).astype(out[name].dtype)
    return out
```

```python
from contextlib import ExitStack

import concourse.bass as bass
from concourse import mybir

P = 128
B, L, D = 4, 512, 512
C, DQ = 256, 128
E, F = 8, 352
KC = D // P
CC = C // P
TB = L // P
TT = B * TB
FCH = [128, 128, 96]
W13, W2C = KC * 2 * F, len(FCH) * D
WC = W13 + W2C
PIECES = [(0, W13 // 2), (W13 // 2, W13 // 2), (W13, W2C)]
QUARTER = 2 * WC // B
RAW = 3 * W2C
RING = 3
RT = (2 * TT * P + E * (P - 1)) // P
EPS = 1e-5

F32, F32R = mybir.dt.float32, mybir.dt.float32r
I32, U32 = mybir.dt.int32, mybir.dt.uint32
ALU = mybir.AluOpType
ACT = mybir.ActivationFunctionType
AX = mybir.AxisListType.X


def flamingo_kernel(nc, x, ctxT, wqk, bqk, gwT, rbias, gates, wall, out, xn_dram, xs_dram, ys_dram):
    x_t = x.rearrange("b (t p) d -> p b t d", p=P)
    out_t = out.rearrange("b (t p) d -> (b t) p d", p=P)
    xn_t = xn_dram.rearrange("(t p) d -> t p d", p=P)
    xs_t = xs_dram.rearrange("(t p) d -> t p d", p=P)
    ys_t = ys_dram.rearrange("(t p) d -> t p d", p=P)

    with ExitStack() as es:
        def sem(name):
            return es.enter_context(nc.semaphore(name))

        place = {"at": (nc.sbuf_base + 31) // 32 * 32}

        def sb(name, shape, dt, at=None):
            n = 4
            for s in shape[1:]:
                n *= s
            off = place["at"] if at is None else at
            t = nc.alloc_sbuf_tensor_at(name, shape, dt, offset=off)
            if at is None:
                place["at"] += (n + 31) // 32 * 32
            return t

        acc = sb("acc", [P, TT * D], F32)
        ident = sb("ident", [P, P], F32)
        gw_f = sb("gw_f", [P, KC * E], F32)
        gw_h = sb("gw_h", [P, KC * E], F32R)
        gw_l = sb("gw_l", [P, KC * E], F32R)
        bias_qk = sb("bias_qk", [P, 2], F32)
        rb = sb("rb", [P, E], F32)
        gate_in = sb("gate_in", [P, 2], F32)
        tg = sb("tg", [P, 2], F32)
        logits = sb("logits", [P, TT * E], F32)
        neg_half = sb("neg_half", [P, TB], F32)
        mv = sb("mv", [P, TB, 2], F32)
        ve = sb("ve", [P, TB], F32)
        rstd = sb("rstd", [P, TB], F32)
        nb = sb("nb", [P, TB], F32)
        mv2 = sb("mv2", [P, TB, 2], F32)
        ve2 = sb("ve2", [P, TB], F32)
        rstd2 = sb("rstd2", [P, TB], F32)
        nb2 = sb("nb2", [P, TB], F32)
        st = sb("st", [P, 2 * TB, 6], F32)
        nmax = sb("nmax", [P, TB], F32)
        esum = sb("esum", [P, TB], F32)
        rsum = sb("rsum", [P, TB], F32)
        raw = sb("raw", [P, RAW], F32)
        ring_h = sb("ring_h", [P, RING * WC], F32R)
        ring_l = sb("ring_l", [P, RING * WC], F32R)
        arena = place["at"]

        place["at"] = arena - 4 * WC
        lnxT_h = sb("lnxT_h", [P, TB, L], F32R)
        lnxT_l = sb("lnxT_l", [P, TB, L], F32R)
        place["at"] = max(place["at"], arena)
        attT_h = sb("attT_h", [P, TB, L], F32R)
        attT_l = sb("attT_l", [P, TB, L], F32R)
        ctx_f = sb("ctx_f", [P, B * CC * L], F32)
        rows = sb("rows", [P, 2, D], F32)
        att = sb("att", [P, 2, L], F32)
        wqk_f = att[:, :, :].rearrange("p a b -> p (a b)")[:, 0:CC * 2 * DQ]
        zero = sb("zero", [P, D], F32)
        top = place["at"]
        place["at"] = arena - 4 * RING * WC - 4 * WC
        ctx_h = sb("ctx_h", [P, CC, L], F32R)
        ctx_l = sb("ctx_l", [P, CC, L], F32R)
        qkx_h = sb("qkx_h", [P, 2, L], F32R)
        qkx_l = sb("qkx_l", [P, 2, L], F32R)
        assert place["at"] <= arena - 4 * RING * WC
        place["at"] = top
        wqk_h = sb("wqk_h", [P, CC, 2 * DQ], F32R)
        wqk_l = sb("wqk_l", [P, CC, 2 * DQ], F32R)
        assert place["at"] <= 229376, place["at"]

        place["at"] = arena
        xs = sb("xs", [P, 2, D], F32)
        xT_h = sb("xT_h", [P, KC, P], F32R)
        xT_l = sb("xT_l", [P, KC, P], F32R)
        silu = sb("silu", [P, F], F32)
        g = sb("g", [P, F], F32)
        gT_h = sb("gT_h", [P, 3, P], F32R)
        gT_l = sb("gT_l", [P, 3, P], F32R)
        ysb = sb("ysb", [P, 2, D], F32)
        xd = sb("xd", [P, 4, D], F32)
        score = sb("score", [P, TT, E], F32)
        sel = sb("sel", [P, TT, E], F32)
        top8 = sb("top8", [P, TT, 8], F32)
        idx8 = sb("idx8", [P, TT, 8], U32)
        idxf = sb("idxf", [P, TT, 2], F32)
        one_hot = [sb(f"one_hot{k}", [P, TT, E], F32) for k in range(2)]
        mask = sb("mask", [P, TT * E], F32R)
        tmp = sb("tmp", [P, TT, E], F32)
        cnt = sb("cnt", [P, TT, E], F32)
        pre = [sb(f"pre{k}", [P, TT, E], F32) for k in range(2)]
        picked = sb("picked", [P, 2, TT], F32)
        wsum = sb("wsum", [P, TT], F32)
        weight = sb("weight", [P, 2, TT], F32)
        ntile = sb("ntile", [P, E], F32)
        first = sb("first", [P, E], F32)
        first_r = sb("first_r", [P, E], F32)
        slot_f = sb("slot_f", [P, TT], F32)
        slot = sb("slot", [P, 2, TT], U32)
        iota_e = sb("iota_e", [P, E], F32)
        iota_t = sb("iota_t", [P, RT + 1], F32)
        iota_k = sb("iota_k", [P, TT], F32)
        below = sb("below", [P, E, E], F32)
        step_r = sb("step_r", [P, E], F32)
        upper_f = sb("upper_f", [P, P], F32)
        upper = sb("upper", [P, P], F32R)
        ones = sb("ones", [P, P], F32R)
        passed = sb("passed", [P, RT + 1, E - 1], F32)
        passed2 = sb("passed2", [P, RT + 1, E - 1], F32)
        tile_f = sb("tile_f", [P, 2, RT + 1], F32)
        tile_tab = sb("tile_tab", [P, 2, RT + 1], I32)
        free_tab = sb("free_tab", [P, E], I32)
        assert place["at"] <= 229376, place["at"]

        bank = [es.enter_context(nc.psum_tensor(f"bank{i}", [P, 512], F32)) for i in range(8)]

        s_const = sem("s_const")
        s_pool_c = sem("s_pool_c")
        s_zero = sem("s_zero")
        s_fill = sem("s_fill")
        s_wqk_h, s_wqk_l = sem("s_wqk_h"), sem("s_wqk_l")
        s_tanh = sem("s_tanh")
        s_x, s_ctx = sem("s_x"), sem("s_ctx")
        s_ctx_h, s_ctx_l = sem("s_ctx_h"), sem("s_ctx_l")
        s_q_ps, s_q_h, s_q_l = sem("s_q_ps"), sem("s_q_h"), sem("s_q_l")
        s_bn1, s_rstd1, s_lnx = sem("s_bn1"), sem("s_rstd1"), sem("s_lnx")
        s_lx_ps, s_lx_h, s_lx_l = sem("s_lx_ps"), sem("s_lx_h"), sem("s_lx_l")
        s_e_ps, s_max, s_exp, s_rsum, s_att = (sem(f"s_{n}") for n in ("e_ps", "max", "exp", "rsum", "att"))
        s_at_ps, s_at_h, s_at_l = sem("s_at_ps"), sem("s_at_h"), sem("s_at_l")
        s_xm_ps, s_x1 = sem("s_xm_ps"), sem("s_x1")
        s_bn2, s_rstd2, s_xn = sem("s_bn2"), sem("s_rstd2"), sem("s_xn")
        s_xn_st = [sem(f"s_xn_st{k}") for k in range(2)]
        s_xt_ps, s_xt_h, s_xt_l = sem("s_xt_ps"), sem("s_xt_h"), sem("s_xt_l")
        s_lg_ps, s_lg = sem("s_lg_ps"), sem("s_lg")
        s_dve, s_pool = sem("s_dve"), sem("s_pool")
        s_score = sem("s_score")
        s_mask, s_rank_ps, s_route = sem("s_mask"), sem("s_rank_ps"), sem("s_route")
        s_xd = [sem(f"s_xd{k}") for k in range(4)]
        s_sc = [sem(f"s_sc{k}") for k in range(4)]
        s_wraw = [sem(f"s_wraw{k}") for k in range(3)]
        s_whi = [sem(f"s_whi{k}") for k in range(3)]
        s_wlo = sem("s_wlo")
        s_xs = [sem(f"s_xs{k}") for k in range(2)]
        s_xT_ps, s_xT_h, s_xT_l = sem("s_xT_ps"), sem("s_xT_h"), sem("s_xT_l")
        s_h1, s_h3, s_silu, s_g = sem("s_h1"), sem("s_h3"), sem("s_silu"), sem("s_g")
        s_gT_ps, s_gT_h, s_gT_l = sem("s_gT_ps"), sem("s_gT_h"), sem("s_gT_l")
        s_y, s_yacc, s_ycp = sem("s_y"), sem("s_yacc"), sem("s_ycp")
        s_yst = [sem(f"s_yst{k}") for k in range(2)]
        s_gy = [sem(f"s_gy{k}") for k in range(4)]
        s_comb = sem("s_comb")
        s_out = sem("s_out")

        b_q, b_e, b_lx, b_at = bank[0:2], bank[2:4], bank[4:6], bank[6:8]
        b_xm, b_xt, b_lg = b_q, b_lx, b_e[0]
        b_h1, b_h3, b_gT, b_xT, b_y = bank[0], bank[1], bank[2], bank[3], bank[4:6]
        b_rank = b_at
        f = lambda ap: ap.bitcast(F32)

        def wait_alone(eng, semaphore, value):
            value = eng.to_reg(value)
            eng.wait_ge(s_pool_c, 2)
            eng.wait_ge(semaphore, value)

        block = es.enter_context(nc.Block())

        @block.sync
        def _(sp):
            ctx_t = ctxT.rearrange("b (c p) l -> p b c l", p=P)

            def load_ctx(b):
                dst = ctx_f[:, b * CC * L:(b + 1) * CC * L].rearrange("p (c l) -> p c l", c=CC)
                sp.dma_start(dst, ctx_t[:, b]).then_inc(s_ctx, 16)

            def load_x(b):
                dst = acc[:, b * TB * D:(b + 1) * TB * D].rearrange("p (t d) -> p t d", t=TB)
                sp.dma_start(dst, x_t[:, b]).then_inc(s_x, 16)

            for k in range(2):
                sp.sem_inc(s_xn_st[k], 16)
            load_ctx(0)
            sp.dma_start(wqk_f.rearrange("p (c n) -> p c n", c=CC), wqk.rearrange("(c p) n -> p c n", p=P)).then_inc(s_const, 16)
            load_x(0)
            sp.dma_start(bias_qk[:, :], bqk).then_inc(s_const, 16)
            sp.dma_start(gw_f[:, :].rearrange("p (c n) -> p c n", c=KC), gwT.rearrange("(c p) n -> p c n", p=P)).then_inc(s_const, 16)
            sp.dma_start(rb[:, :], rbias).then_inc(s_const, 16)
            sp.dma_start(gate_in[:, :], gates).then_inc(s_const, 16)
            for b in range(1, B):
                sp.wait_ge(s_ctx, 16 * b)
                load_ctx(b)
                sp.wait_ge(s_x, 16 * b)
                load_x(b)
            sp.wait_ge(s_zero, 1)
            sp.dma_start(xs_dram.rearrange("(t p) d -> p t d", p=P),
                         zero[:, :].rearrange("p (o d) -> p o d", o=1).broadcast_to([P, RT, D])).then_inc(s_fill, 16)
            with sp.Fori(0, B) as b:
                for t in range(TB):
                    sp.wait_ge(s_xn, b * TB + (t + 1))
                    sp.dma_start(xn_t[bass.ds(b * TB + t, 1)].rearrange("o p d -> p o d"),
                                 rows[:, t % 2:t % 2 + 1, :]).then_inc(s_xn_st[t % 2], 16)
            for k in range(2):
                sp.wait_ge(s_xn_st[k], 16 + 16 * TT // 2)

            def load_xs(src, t, k):
                sp.dma_start(xs[:, k:k + 1, :], src[bass.ds(t, 1)].rearrange("o p d -> p o d")).then_inc(s_xs[k], 16)

            sp.wait_ge(s_lg, B)
            for n in range(2):
                load_xs(xn_t, n, n)
            with sp.Fori(1, TT // 2) as j:
                for k in range(2):
                    sp.wait_ge(s_xT_ps, j * 2 + (k - 1))
                    load_xs(xn_t, j * 2 + k, k)
            for k in range(4):
                sp.wait_ge(s_sc[k], 2 * 16 * TT // 4)
            for t in range(4):
                sp.wait_ge(s_xT_ps, TT + t - 1)
                load_xs(xs_t, t, t % 2)

            def store_y(t, k):
                sp.wait_ge(s_ycp, t + 3)
                sp.dma_start(ys_t[bass.ds(t, 1)].rearrange("o p d -> p o d"), ysb[:, k:k + 1, :]).then_inc(s_yst[k], 16)

            with sp.Fori(0, (RT - 5) // 2) as j:
                for k in range(2):
                    sp.wait_ge(s_xT_ps, j * 2 + (TT + k + 3))
                    load_xs(xs_t, j * 2 + (k + 4), k)
                    store_y(j * 2 + k, k)
            for t in range((RT - 5) // 2 * 2, RT):
                if t + 4 < RT:
                    sp.wait_ge(s_xT_ps, TT + t + 3)
                    load_xs(xs_t, t + 4, t % 2)
                store_y(t, t % 2)
            for t in range(TT):
                sp.wait_ge(s_comb, t + 1)
                sp.dma_start(out_t[t], acc[:, t * D:(t + 1) * D]).then_inc(s_out, 16)
            sp.wait_ge(s_out, 16 * TT)

        @block.gpsimd
        def _(pool):
            gp = nc.gpsimd

            for k in range(2):
                pool.sem_inc(s_yst[k], 16)
            gp.memset(ident[:, :], 0.0).then_inc(s_pool_c, 1)
            gp.memset(zero[:, :], 0.0).then_inc(s_zero, 1)
            pool.wait_ge(s_pool_c, 1)
            gp.affine_select(out=ident[:, :], in_=ident[:, :], compare_op=ALU.not_equal, fill=1.0,
                             base=0, pattern=[[-1, P]], channel_multiplier=1).then_inc(s_pool_c, 1)
            gp.memset(neg_half[:, :], -0.5).then_inc(s_pool_c, 1)
            with pool.Fori(0, B) as b:
                HQ = QUARTER // 2
                for k in range(2):
                    wait_alone(pool, s_pool_c, b + 3)
                    part = bass.ds(b * QUARTER + k * HQ, HQ)
                    pool.dma_start(raw[:, k * HQ:(k + 1) * HQ], wall[:, part]).then_inc(s_wraw[k], 16)
                    pool.dma_start(ring_h[:, part], wall[:, part]).then_inc(s_whi[k], 16)
                wait_alone(pool, s_bn1, b + 1)
                gp.tensor_scalar(ve[:, :], mv[:, :, 1], EPS, None, ALU.add).then_inc(s_pool, 1)
                gp.tensor_scalar(mv[:, :, 0], mv[:, :, 0], -1.0, None, ALU.mult).then_inc(s_pool, 1)
                pool.wait_ge(s_pool, b * 9 + 2)
                gp.tensor_tensor(rstd[:, :], ve[:, :], neg_half[:, :], ALU.pow).then_inc(s_pool, 1)
                pool.wait_ge(s_pool, b * 9 + 3)
                gp.tensor_tensor(nb[:, :], mv[:, :, 0], rstd[:, :], ALU.mult).then_inc(s_rstd1, 1)
                pool.wait_ge(s_ctx_h, b + 1)
                gp.tensor_tensor(ctx_l[:, :, :].rearrange("p c l -> p (c l)"),
                                 ctx_f[:, bass.ds(b * CC * L, CC * L)],
                                 f(ctx_h[:, :, :].rearrange("p c l -> p (c l)")), ALU.subtract).then_inc(s_ctx_l, 1)
                for k in range(2):
                    pool.wait_ge(s_wraw[k], b * 16 + 16)
                    pool.wait_ge(s_whi[k], b * 16 + 16)
                    part = bass.ds(b * QUARTER + k * HQ, HQ)
                    o = gp.tensor_tensor(ring_l[:, part], raw[:, k * HQ:(k + 1) * HQ], f(ring_h[:, part]), ALU.subtract)
                o.then_inc(s_pool_c, 1)
                for t in range(0, TB, 2):
                    two = slice(t, t + 2)
                    wait_alone(pool, s_bn2, b * TB + (t + 2))
                    gp.tensor_scalar(ve2[:, two], mv2[:, two, 1], EPS, None, ALU.add).then_inc(s_pool, 1)
                    gp.tensor_scalar(mv2[:, two, 0], mv2[:, two, 0], -1.0, None, ALU.mult).then_inc(s_pool, 1)
                    pool.wait_ge(s_pool, b * 9 + (5 + 3 * (t // 2)))
                    gp.tensor_tensor(rstd2[:, two], ve2[:, two], neg_half[:, two], ALU.pow).then_inc(s_pool, 1)
                    pool.wait_ge(s_pool, b * 9 + (6 + 3 * (t // 2)))
                    gp.tensor_tensor(nb2[:, two], mv2[:, two, 0], rstd2[:, two], ALU.mult).then_inc(s_rstd2, 1)

            pool.wait_ge(s_lg, B)
            pool.wait_ge(s_fill, 16)
            pool.wait_ge(s_xn_st[0], 16 + 16 * TT // 2)
            pool.wait_ge(s_xn_st[1], 16 + 16 * TT // 2)
            imprecise = dict(channel_multiplier=0, allow_small_or_imprecise_dtypes=True)
            gp.iota(iota_e[:, :], pattern=[[1, E]], base=0, **imprecise)
            gp.iota(iota_t[:, :], pattern=[[1, RT + 1]], base=0, **imprecise)
            gp.iota(iota_k[:, :], pattern=[[P, TT]], base=0, **imprecise)
            gp.memset(below[:, :, :], 1.0).then_inc(s_pool_c, 1)
            gp.memset(step_r[:, :], 1.0).then_inc(s_pool_c, 1)
            gp.memset(upper_f[:, :], 1.0).then_inc(s_pool_c, 1)
            pool.wait_ge(s_pool_c, 3 + B + 3)
            for e in range(1, E):
                if (e + 2) % RING == 0:
                    gp.memset(step_r[:, e - 1:e], 1.0 - RING)
            gp.affine_select(out=below[:, :, :], in_=below[:, :, :], compare_op=ALU.is_gt, fill=0.0,
                             base=0, pattern=[[1, E], [-1, E]], channel_multiplier=0)
            gp.affine_select(out=upper_f[:, :], in_=upper_f[:, :], compare_op=ALU.is_gt, fill=0.0,
                             base=0, pattern=[[1, P]], channel_multiplier=-1).then_inc(s_pool_c, 1)

            def scatter(t):
                if t == 0:
                    pool.wait_ge(s_route, 1)
                pool.wait_ge(s_xd[t % 4], 16 * (t // 4 + 1))
                for k in range(2):
                    pool.indirect_dma_start(xs_dram, bass.IndirectOffsetOnAxis(slot[:, k, t:t + 1], 0),
                                            xd[:, t % 4, :], None).then_inc(s_sc[t % 4], 16)

            for t in range(TT):
                k = t % 4
                if t >= 4:
                    pool.wait_ge(s_sc[k], 32 * (t // 4))
                pool.dma_start(xd[:, k, :], xn_t[t]).then_inc(s_xd[k], 16)
                if t >= 3:
                    scatter(t - 3)
            for t in range(TT - 3, TT):
                scatter(t)

            def load_raw(e, n):
                lo, w = PIECES[n]
                pool.dma_start(raw[:, n * W2C:n * W2C + w], wall[:, bass.ds(e * WC + lo, w)]).then_inc(s_wraw[n], 16)

            for n in range(3):
                load_raw(2, n)
            r0 = [16 * B, 16 * B, 0]

            def split_weights(e, r, k, more):
                for n, (lo, w) in enumerate(PIECES):
                    pool.dma_start(ring_h[:, bass.ds(r * WC + lo, w)], wall[:, bass.ds(e * WC + lo, w)]).then_inc(s_whi[n], 16)
                for n, (lo, w) in enumerate(PIECES):
                    pool.wait_ge(s_wraw[n], k * 16 + (r0[n] + 16))
                    pool.wait_ge(s_whi[n], k * 16 + (r0[n] + 16))
                    part = bass.ds(r * WC + lo, w)
                    gp.tensor_tensor(ring_l[:, part], raw[:, n * W2C:n * W2C + w], f(ring_h[:, part]),
                                     ALU.subtract).then_inc(s_wlo, 1)
                    if more:
                        pool.wait_ge(s_wlo, k * 3 + (n + 1))
                        load_raw(e + 1, n)

            split_weights(2, 2, 0, True)
            pool.wait_ge(s_y, TT)
            split_weights(3, 0, 1, True)
            split_weights(4, 1, 2, True)
            for e in range(5, E + 2):
                freed = pool.value_load(free_tab[0:1, e - 2:e - 1], min_val=1, max_val=TT + RT)
                wait_alone(pool, s_y, freed)
                split_weights(e, e % RING, e - 2, e < E + 1)

            pool.wait_ge(s_yst[0], 16 + 16 * ((RT + 1) // 2))
            pool.wait_ge(s_yst[1], 16 + 16 * (RT // 2))
            for t in range(TT):
                if t >= 2:
                    pool.wait_ge(s_comb, t - 1)
                for k in range(2):
                    q = 2 * (t % 2) + k
                    pool.indirect_dma_start(xd[:, q, :], None, ys_dram,
                                            bass.IndirectOffsetOnAxis(slot[:, k, t:t + 1], 0)).then_inc(s_gy[q], 16)

        @block.scalar
        def _(act):
            a = nc.scalar
            act.wait_ge(s_const, 16 * 5)
            a.activation(wqk_h[:, :, :].rearrange("p c n -> p (c n)"), wqk_f, ACT.Copy).then_inc(s_wqk_h, 1)
            a.activation(gw_h[:, :], gw_f[:, :], ACT.Copy).then_inc(s_wqk_h, 1)
            a.activation(tg[:, :], gate_in[:, :], ACT.Tanh).then_inc(s_tanh, 1)
            with act.Fori(0, B) as b:
                act.wait_ge(s_ctx, b * 16 + 16)
                a.activation(ctx_h[:, :, :].rearrange("p c l -> p (c l)"),
                             ctx_f[:, bass.ds(b * CC * L, CC * L)], ACT.Copy).then_inc(s_ctx_h, 1)
                for k in range(2):
                    act.wait_ge(s_q_ps, b * 2 + (k + 1))
                    a.activation(qkx_h[:, k, :], b_q[k][:, :], ACT.Identity, bias=bias_qk[:, k:k + 1]).then_inc(s_q_h, 1)

                def normalise(t):
                    if t == 0:
                        wait_alone(act, s_rstd1, b + 1)
                    if t < 2:
                        wait_alone(act, s_xn_st[t], b * 32 + 16)
                    a.activation(rows[:, t % 2, :], acc[:, bass.ds(b * TB * D + t * D, D)], ACT.Identity,
                                 bias=nb[:, t:t + 1], scale=rstd[:, t:t + 1]).then_inc(s_lnx, 1)

                def lnxT_hi(t):
                    act.wait_ge(s_lx_ps, b * TB + (t + 1))
                    a.activation(lnxT_h[:, :, t * P:(t + 1) * P],
                                 b_lx[t % 2][:, :].rearrange("p (c l) -> p c l", c=TB), ACT.Copy).then_inc(s_lx_h, 1)

                def exp(t):
                    act.wait_ge(s_max, b * TB + (t + 1))
                    a.activation(att[:, t % 2, :], b_e[t % 2][:, :], ACT.Exp, bias=nmax[:, t:t + 1],
                                 accum_out=esum[:, t:t + 1]).then_inc(s_exp, 1)

                def divide(t):
                    act.wait_ge(s_rsum, b * TB + (t + 1))
                    a.activation(att[:, t % 2, :], att[:, t % 2, :], ACT.Copy, scale=rsum[:, t:t + 1]).then_inc(s_att, 1)

                def attT_hi(t):
                    act.wait_ge(s_at_ps, b * TB + (t + 1))
                    a.activation(attT_h[:, :, t * P:(t + 1) * P],
                                 b_at[t % 2][:, :].rearrange("p (c l) -> p c l", c=TB), ACT.Copy).then_inc(s_at_h, 1)

                normalise(0)
                normalise(1)
                lnxT_hi(0)
                exp(0)
                lnxT_hi(1)
                exp(1)
                divide(0)
                normalise(2)
                attT_hi(0)
                lnxT_hi(2)
                exp(2)
                divide(1)
                normalise(3)
                attT_hi(1)
                lnxT_hi(3)
                exp(3)
                divide(2)
                attT_hi(2)
                divide(3)
                attT_hi(3)

                def normalise2(t):
                    if t % 2 == 0:
                        wait_alone(act, s_rstd2, b * 2 + (t // 2 + 1))
                    if t >= 2:
                        wait_alone(act, s_xn_st[t % 2], b * 32 + 32)
                    a.activation(rows[:, t % 2, :], acc[:, bass.ds(b * TB * D + t * D, D)], ACT.Identity,
                                 bias=nb2[:, t:t + 1], scale=rstd2[:, t:t + 1]).then_inc(s_xn, 1)

                def rowsT_hi(t):
                    act.wait_ge(s_xt_ps, b * TB + (t + 1))
                    a.activation(qkx_h[:, t % 2, :], b_xt[t % 2][:, :], ACT.Copy).then_inc(s_xt_h, 1)

                normalise2(0)
                normalise2(1)
                rowsT_hi(0)
                rowsT_hi(1)
                normalise2(2)
                normalise2(3)
                rowsT_hi(2)
                rowsT_hi(3)

            act.wait_ge(s_lg, B)
            act.wait_ge(s_xn_st[0], 16 + 16 * TT // 2)
            act.wait_ge(s_xn_st[1], 16 + 16 * TT // 2)
            act.wait_ge(s_fill, 16)
            a.activation(score[:, :, :].rearrange("p t e -> p (t e)"), logits[:, :], ACT.Sigmoid).then_inc(s_score, 1)

            def hidden_act(u):
                act.wait_ge(s_h1, u + 1)
                act.wait_ge(s_g, u + 1)
                a.activation(silu[:, :], b_h1[:, 0:F], ACT.Silu).then_inc(s_silu, 1)

            def gT_hi(u):
                act.wait_ge(s_gT_ps, u + 1)
                a.activation(gT_h[:, :, :].rearrange("p c n -> p (c n)")[:, 0:2 * P], b_gT[:, 0:2 * P], ACT.Copy)
                a.activation(gT_h[0:FCH[2], 2, :], b_gT[0:FCH[2], 2 * P:3 * P], ACT.Copy).then_inc(s_gT_h, 1)

            def xT_hi(n):
                act.wait_ge(s_xT_ps, n + 1)
                a.activation(xT_h[:, :, :].rearrange("p c n -> p (c n)"), b_xT[:, :], ACT.Copy).then_inc(s_xT_h, 1)

            act.sem_inc(s_g, 1)
            act.sem_inc(s_ycp, 2)
            xT_hi(0)
            hidden_act(0)

            def shared_pair(j, last):
                for q in range(4):
                    u = j * 4 + q
                    hidden_act(u + 1)
                    gT_hi(u)
                    if q % 2 == 0:
                        xT_hi(j * 2 + (q // 2 + 1))
                    elif last and q == 3:
                        xT_hi(TT + 1)

            with act.Fori(0, TT // 2 - 1) as j:
                shared_pair(j, False)
            shared_pair(TT // 2 - 1, True)

            def routed(t, k, j, nxt, turn):
                if nxt:
                    hidden_act(t + (2 * TT + 1))
                gT_hi(t + 2 * TT)
                if turn:
                    xT_hi(t + (TT + 2))
                act.wait_ge(s_y, t + (TT + 1))
                act.wait_ge(s_yst[k], j * 16 + 16)
                a.activation(ysb[:, k, :], b_y[k][:, :], ACT.Copy).then_inc(s_ycp, 1)

            with act.Fori(0, (RT - 2) // 2) as j:
                for k in range(2):
                    routed(j * 2 + k, k, j, True, True)
            for t in range((RT - 2) // 2 * 2, RT):
                routed(t, t % 2, t // 2, t + 1 < RT, t + 2 < RT)

        @block.vector
        def _(dve):
            v = nc.vector
            chain = {"n": 0}

            def link(ins, base=0):
                chain["n"] += 1
                ins.then_inc(s_dve, 1)
                if isinstance(base, int):
                    dve.wait_ge(s_dve, base + chain["n"])
                else:
                    wait_alone(dve, s_dve, base + chain["n"])

            dve.wait_ge(s_wqk_h, 2)
            v.tensor_tensor(wqk_l[:, :, :].rearrange("p c n -> p (c n)"), wqk_f,
                            f(wqk_h[:, :, :].rearrange("p c n -> p (c n)")), ALU.subtract).then_inc(s_wqk_l, 1)
            v.tensor_tensor(gw_l[:, :], gw_f[:, :], f(gw_h[:, :]), ALU.subtract).then_inc(s_wqk_l, 1)
            dve.wait_ge(s_tanh, 1)
            per_b = 1 + TB
            with dve.Fori(0, B) as b:
                chain["n"] = 0
                base = b * per_b
                tile = lambda t: acc[:, bass.ds(b * TB * D + t * D, D)]
                wait_alone(dve, s_x, b * 16 + 16)
                for t in range(TB):
                    o = v.bn_stats(st[:, t, :], tile(t))
                link(o, base)
                for t in range(TB):
                    o = v.bn_aggr(mv[:, t, :], st[:, t, :])
                o.then_inc(s_bn1, 1)
                for k in range(2):
                    dve.wait_ge(s_q_h, b * 2 + (k + 1))
                    v.scalar_tensor_tensor(out=qkx_l[:, k, :], in0=b_q[k][:, :], scalar=bias_qk[:, k:k + 1],
                                           in1=f(qkx_h[:, k, :]), op0=ALU.add, op1=ALU.subtract).then_inc(s_q_l, 1)

                def neg_max(t):
                    dve.wait_ge(s_e_ps, b * TB + (t + 1))
                    v.tensor_reduce(nmax[:, t:t + 1], b_e[t % 2][:, :], AX, ALU.max, negate=True).then_inc(s_max, 1)

                def lnxT_lo(t):
                    dve.wait_ge(s_lx_h, b * TB + (t + 1))
                    v.tensor_tensor(lnxT_l[:, :, t * P:(t + 1) * P], b_lx[t % 2][:, :].rearrange("p (c l) -> p c l", c=TB),
                                    f(lnxT_h[:, :, t * P:(t + 1) * P]), ALU.subtract).then_inc(s_lx_l, 1)

                def recip(t):
                    dve.wait_ge(s_exp, b * TB + (t + 1))
                    v.reciprocal(rsum[:, t:t + 1], esum[:, t:t + 1]).then_inc(s_rsum, 1)

                def attT_lo(t):
                    dve.wait_ge(s_at_h, b * TB + (t + 1))
                    v.tensor_tensor(attT_l[:, :, t * P:(t + 1) * P], b_at[t % 2][:, :].rearrange("p (c l) -> p c l", c=TB),
                                    f(attT_h[:, :, t * P:(t + 1) * P]), ALU.subtract).then_inc(s_at_l, 1)

                neg_max(0)
                lnxT_lo(0)
                neg_max(1)
                recip(0)
                lnxT_lo(1)
                recip(1)
                attT_lo(0)
                neg_max(2)
                lnxT_lo(2)
                recip(2)
                attT_lo(1)
                neg_max(3)
                lnxT_lo(3)
                recip(3)
                attT_lo(2)
                attT_lo(3)
                for t in range(TB):
                    dve.wait_ge(s_xm_ps, b * TB + (t + 1))
                    o = v.scalar_tensor_tensor(out=tile(t), in0=b_xm[t % 2][:, :], scalar=tg[:, 0:1], in1=tile(t),
                                               op0=ALU.mult, op1=ALU.add)
                    o.then_inc(s_x1, 1)
                    wait_alone(dve, s_x1, b * TB + (t + 1))
                    link(v.bn_stats(st[:, TB + t, :], tile(t)), base)
                    v.bn_aggr(mv2[:, t, :], st[:, TB + t, :]).then_inc(s_bn2, 1)
                for t in range(TB):
                    dve.wait_ge(s_xt_h, b * TB + (t + 1))
                    v.tensor_tensor(qkx_l[:, t % 2, :], b_xt[t % 2][:, :], f(qkx_h[:, t % 2, :]), ALU.subtract).then_inc(s_xt_l, 1)
                dve.wait_ge(s_lg_ps, b + 1)
                v.tensor_copy(logits[:, bass.ds(b * TB * E, TB * E)], b_lg[:, 0:TB * E]).then_inc(s_lg, 1)

            base = B * per_b
            chain["n"] = 0

            def over(ap, n):
                return ap.rearrange("p (o k) -> p o k", o=1).broadcast_to([P, n, ap.shape[1]])

            dve.wait_ge(s_score, 1)
            dve.wait_ge(s_pool_c, 3 + B + 4)
            link(v.tensor_tensor(sel[:, :, :], score[:, :, :], over(rb[:, :], TT), ALU.add), base)
            for t in range(TT):
                o = v.max(top8[:, t, :], sel[:, t, :])
            link(o, base)
            for t in range(TT):
                o = v.max_index(idx8[:, t, :], top8[:, t, :], sel[:, t, :])
            link(o, base)
            link(v.tensor_copy(idxf[:, :, :], idx8[:, :, 0:2]), base)
            ie = over(iota_e[:, :], TT)
            for k in range(2):
                o = v.tensor_tensor(one_hot[k][:, :, :], ie, idxf[:, :, k:k + 1].broadcast_to([P, TT, E]), ALU.is_equal)
            link(o, base)
            v.tensor_copy(upper[:, :], upper_f[:, :])
            v.memset(f(ones[:, :]), 1.0)
            v.tensor_tensor(mask[:, :].rearrange("p (t e) -> p t e", t=TT), one_hot[0][:, :, :], one_hot[1][:, :, :], ALU.add).then_inc(s_mask, 1)
            for k in range(2):
                link(v.tensor_tensor(tmp[:, :, :], one_hot[k][:, :, :], score[:, :, :], ALU.mult), base)
                link(v.tensor_reduce(picked[:, k, :], tmp[:, :, :], AX, ALU.add), base)
            link(v.tensor_tensor(wsum[:, :], picked[:, 0, :], picked[:, 1, :], ALU.add), base)
            link(v.tensor_scalar(wsum[:, :], wsum[:, :], 1e-12, None, ALU.max), base)
            link(v.reciprocal(wsum[:, :], wsum[:, :]), base)
            for k in range(2):
                link(v.tensor_tensor(picked[:, k, :], picked[:, k, :], wsum[:, :], ALU.mult), base)
                link(v.tensor_scalar(weight[:, k, :], picked[:, k, :], tg[:, 1:2], None, ALU.mult), base)
            dve.wait_ge(s_rank_ps, 1)
            v.tensor_copy(cnt[:, :, :].rearrange("p t e -> p (t e)"), b_rank[1][:, 0:TT * E])
            link(v.tensor_copy(pre[0][:, :, :].rearrange("p t e -> p (t e)"), b_rank[1][:, 0:TT * E]), base)
            s, k = 1, 0
            while s < TT:
                v.tensor_copy(pre[1 - k][:, 0:s, :], pre[k][:, 0:s, :])
                link(v.tensor_tensor(pre[1 - k][:, s:, :], pre[k][:, s:, :], pre[k][:, 0:TT - s, :], ALU.add), base)
                s, k = 2 * s, 1 - k
            incl = pre[k]
            total = incl[:, TT - 1:TT, :].rearrange("p o e -> p e o")
            cmp = tmp[:, :, :].rearrange("p t e -> p (t e)").rearrange("p (e t) -> p e t", e=E)
            link(v.tensor_tensor(cmp, total.broadcast_to([P, E, TT]), over(iota_k[:, :], E), ALU.is_gt), base)
            link(v.tensor_reduce(ntile[:, :], cmp, AX, ALU.add), base)
            less = tmp[:, 0:E, :]
            link(v.tensor_tensor(less, below[:, :, :], over(ntile[:, :], E), ALU.mult), base)
            link(v.tensor_reduce(first[:, :], less, AX, ALU.add), base)
            link(v.tensor_scalar(first_r[:, :], first[:, :], float(P), None, ALU.mult), base)
            link(v.tensor_tensor(cnt[:, :, :], incl[:, :, :], cnt[:, :, :], ALU.subtract), base)
            link(v.tensor_tensor(cnt[:, :, :], cnt[:, :, :], over(first_r[:, :], TT), ALU.add), base)
            link(v.tensor_tensor(cnt[:, :, :].rearrange("p t e -> p (t e)"), b_rank[0][:, 0:TT * E],
                                 cnt[:, :, :].rearrange("p t e -> p (t e)"), ALU.add), base)
            for k in range(2):
                link(v.tensor_tensor(tmp[:, :, :], one_hot[k][:, :, :], cnt[:, :, :], ALU.mult), base)
                link(v.tensor_reduce(slot_f[:, :], tmp[:, :, :], AX, ALU.add), base)
                link(v.tensor_copy(slot[:, k, :], slot_f[:, :]), base)
            fe = over(first[:, 1:E], RT + 1)
            link(v.tensor_tensor(passed[:, :, :], iota_t[:, :].rearrange("p (t o) -> p t o", o=1).broadcast_to([P, RT + 1, E - 1]), fe, ALU.is_ge), base)
            link(v.tensor_reduce(tile_f[:, 1, :], passed[:, :, :], AX, ALU.add), base)
            link(v.tensor_tensor(passed2[:, :, :], passed[:, :, :],
                                 over(step_r[:, 0:E - 1], RT + 1), ALU.mult), base)
            link(v.tensor_reduce(tile_f[:, 0, :], passed2[:, :, :], AX, ALU.add), base)
            link(v.tensor_scalar(tile_f[:, 0, :], tile_f[:, 0, :], float(WC), 2.0 * WC, ALU.mult, ALU.add), base)
            link(v.tensor_scalar(tile_f[:, 1, :], tile_f[:, 1, :], 3.0, 3.0, ALU.mult, ALU.add), base)
            link(v.tensor_copy(tile_tab[:, :, :], tile_f[:, :, :]), base)
            link(v.tensor_scalar(first_r[:, :], first[:, :], float(TT), None, ALU.add), base)
            v.tensor_copy(free_tab[:, 2:E], first_r[:, 0:E - 2])
            link(v.tensor_copy(free_tab[:, 0:2], first_r[:, 0:2]), base)
            dve.sem_inc(s_route, 1)

            def xT_lo(n):
                dve.wait_ge(s_xT_h, n + 1)
                v.tensor_tensor(xT_l[:, :, :].rearrange("p c n -> p (c n)"), b_xT[:, :],
                                f(xT_h[:, :, :].rearrange("p c n -> p (c n)")), ALU.subtract).then_inc(s_xT_l, 1)

            def product(u):
                dve.wait_ge(s_silu, u + 1)
                dve.wait_ge(s_h3, u + 1)
                v.tensor_tensor(g[:, :], silu[:, :], b_h3[:, 0:F], ALU.mult).then_inc(s_g, 1)

            def gT_lo(u):
                dve.wait_ge(s_gT_h, u + 1)
                v.tensor_tensor(gT_l[:, :, :].rearrange("p c n -> p (c n)")[:, 0:2 * P], b_gT[:, 0:2 * P],
                                f(gT_h[:, :, :].rearrange("p c n -> p (c n)")[:, 0:2 * P]), ALU.subtract)
                v.tensor_tensor(gT_l[0:FCH[2], 2, :], b_gT[0:FCH[2], 2 * P:3 * P], f(gT_h[0:FCH[2], 2, :]),
                                ALU.subtract).then_inc(s_gT_l, 1)

            dve.sem_inc(s_yacc, 2)
            xT_lo(0)
            product(0)

            def shared_pair(j, last):
                for q in range(4):
                    u = j * 4 + q
                    gT_lo(u)
                    product(u + 1)
                    if q % 2 == 0:
                        xT_lo(j * 2 + (q // 2 + 1))
                    elif last and q == 3:
                        xT_lo(TT + 1)
                    if q % 2:
                        n, k = j * 2 + q // 2, q // 2
                        tile = acc[:, bass.ds(j * 2 * D + k * D, D)]
                        dve.wait_ge(s_y, n + 1)
                        v.scalar_tensor_tensor(out=tile, in0=b_y[k][:, :], scalar=tg[:, 1:2], in1=tile,
                                               op0=ALU.mult, op1=ALU.add).then_inc(s_yacc, 1)

            with dve.Fori(0, TT // 2 - 1) as j:
                shared_pair(j, False)
            shared_pair(TT // 2 - 1, True)

            def routed(t, nxt, turn):
                gT_lo(t + 2 * TT)
                if nxt:
                    product(t + (2 * TT + 1))
                if turn:
                    xT_lo(t + (TT + 2))

            with dve.Fori(0, (RT - 2) // 2) as j:
                for k in range(2):
                    routed(j * 2 + k, True, True)
            for t in range((RT - 2) // 2 * 2, RT):
                routed(t, t + 1 < RT, t + 2 < RT)

            for t in range(TT):
                tile = acc[:, t * D:(t + 1) * D]
                for k in range(2):
                    q = 2 * (t % 2) + k
                    dve.wait_ge(s_gy[q], 16 * (t // 2 + 1))
                    o = v.scalar_tensor_tensor(out=tile, in0=xd[:, q, :], scalar=weight[:, k, t:t + 1], in1=tile,
                                               op0=ALU.mult, op1=ALU.add)
                    if k == 0:
                        link(o, base)
                o.then_inc(s_comb, 1)

        @block.tensor
        def _(pe):
            t_ = nc.tensor

            def product3(out, pairs):
                n = 0
                for sh, sl, mh, ml in pairs:
                    for s, m in ((sh, mh), (sh, ml), (sl, mh)):
                        o = t_.matmul(out, s, m, start=(n == 0), stop=(n == 3 * len(pairs) - 1))
                        n += 1
                return o

            pe.wait_ge(s_wqk_l, 2)
            pe.wait_ge(s_pool_c, 3)
            with pe.Fori(0, B) as b:
                pe.wait_ge(s_ctx_l, b + 1)
                for k in range(2):
                    cols = slice(k * DQ, (k + 1) * DQ)
                    product3(b_q[k][:, :], [(wqk_h[:, c, cols], wqk_l[:, c, cols], ctx_h[:, c, :], ctx_l[:, c, :])
                                            for c in range(CC)]).then_inc(s_q_ps, 1)

                def turn(dst, src, s):
                    for c in range(4):
                        o = t_.transpose(dst[:, c * P:(c + 1) * P], src[:, c * P:(c + 1) * P], ident[:, :])
                    o.then_inc(s, 1)

                def turn_lnx(t):
                    pe.wait_ge(s_lnx, b * TB + (t + 1))
                    if t >= 2:
                        pe.wait_ge(s_lx_l, b * TB + (t - 1))
                    turn(b_lx[t % 2], rows[:, t % 2, :], s_lx_ps)

                def energy(t):
                    if t == 0:
                        pe.wait_ge(s_q_l, b * 2 + 2)
                    if t >= 2:
                        pe.wait_ge(s_exp, b * TB + (t - 1))
                    rs = slice(t * P, (t + 1) * P)
                    product3(b_e[t % 2][:, :], [(qkx_h[:, 0, rs], qkx_l[:, 0, rs], qkx_h[:, 1, :], qkx_l[:, 1, :])]).then_inc(s_e_ps, 1)

                def turn_att(t):
                    pe.wait_ge(s_att, b * TB + (t + 1))
                    if t >= 2:
                        pe.wait_ge(s_at_l, b * TB + (t - 1))
                    turn(b_at[t % 2], att[:, t % 2, :], s_at_ps)

                turn_lnx(0)
                turn_lnx(1)
                energy(0)
                energy(1)
                turn_att(0)
                turn_lnx(2)
                energy(2)
                turn_att(1)
                turn_lnx(3)
                energy(3)
                turn_att(2)
                turn_att(3)
                pe.wait_ge(s_lx_l, b * TB + TB)
                pe.wait_ge(s_at_l, b * TB + TB)
                for t in range(TB):
                    if t >= 2:
                        pe.wait_ge(s_x1, b * TB + (t - 1))
                    rs = slice(t * P, (t + 1) * P)
                    product3(b_xm[t % 2][:, :], [(lnxT_h[:, c, rs], lnxT_l[:, c, rs], attT_h[:, c, :], attT_l[:, c, :])
                                                 for c in range(TB)]).then_inc(s_xm_ps, 1)

                def turn_rows(t):
                    pe.wait_ge(s_xn, b * TB + (t + 1))
                    turn(b_xt[t % 2], rows[:, t % 2, :], s_xt_ps)

                def router(t):
                    pe.wait_ge(s_xt_l, b * TB + (t + 1))
                    o = product3(b_lg[:, t * E:(t + 1) * E],
                                 [(qkx_h[:, t % 2, c * P:(c + 1) * P], qkx_l[:, t % 2, c * P:(c + 1) * P],
                                   gw_h[:, c * E:(c + 1) * E], gw_l[:, c * E:(c + 1) * E]) for c in range(KC)])
                    if t == TB - 1:
                        o.then_inc(s_lg_ps, 1)

                turn_rows(0)
                turn_rows(1)
                router(0)
                turn_rows(2)
                router(1)
                turn_rows(3)
                router(2)
                router(3)

            pe.wait_ge(s_mask, 1)
            t_.matmul(b_rank[0][:, 0:TT * E], upper[:, :], mask[:, :], start=True, stop=True)
            t_.matmul(b_rank[1][:, 0:TT * E], ones[:, :], mask[:, :], start=True, stop=True).then_inc(s_rank_ps, 1)

            def turn_x(k, landed):
                pe.wait_ge(s_xs[k], landed)
                for c in range(KC):
                    o = t_.transpose(b_xT[:, c * P:(c + 1) * P], xs[:, k, c * P:(c + 1) * P], ident[:, :])
                o.then_inc(s_xT_ps, 1)

            def up(which, r):
                dst = (b_h1, b_h3)[which]
                pairs = []
                for c in range(KC):
                    lo = c * 2 * F + which * F
                    pairs.append((xT_h[:, c, :], xT_l[:, c, :], ring_h[:, bass.ds(r + lo, F)], ring_l[:, bass.ds(r + lo, F)]))
                product3(dst[:, 0:F], pairs).then_inc((s_h1, s_h3)[which], 1)

            def turn_g(u):
                pe.wait_ge(s_g, u + 2)
                for c, w in enumerate(FCH):
                    o = t_.transpose(b_gT[0:w, c * P:(c + 1) * P], g[:, c * P:c * P + w], ident[:, :])
                o.then_inc(s_gT_ps, 1)

            def down(u, r, k, start, stop):
                pe.wait_ge(s_gT_l, u + 1)
                dst = b_y[k][:, :]
                n, last = 0, 3 * len(FCH) - 1
                for c, w in enumerate(FCH):
                    lo = W13 + c * D
                    mh, ml = ring_h[0:w, bass.ds(r + lo, D)], ring_l[0:w, bass.ds(r + lo, D)]
                    for s, m in ((gT_h[0:w, c, :], mh), (gT_h[0:w, c, :], ml), (gT_l[0:w, c, :], mh)):
                        o = t_.matmul(dst, s, m, start=(start and n == 0), stop=(stop and n == last))
                        n += 1
                return o

            pe.wait_ge(s_pool_c, 3 + B)
            turn_x(0, 16)
            pe.wait_ge(s_xT_l, 1)
            up(0, 0)
            up(1, 0)

            def shared_pair(j, last):
                for q in range(4):
                    u = j * 4 + q
                    nxt = (1 - q % 2) * WC
                    if last and q == 3:
                        nxt = pe.value_load(tile_tab[0:1, 0, 0:1], min_val=0, max_val=(RING - 1) * WC)
                        w = pe.value_load(tile_tab[0:1, 1, 0:1], min_val=3, max_val=3 * E)
                    if q % 2:
                        pe.wait_ge(s_xT_l, j * 2 + (q // 2 + 2))
                    pe.wait_ge(s_silu, u + 1)
                    if last and q == 3:
                        pe.wait_ge(s_wlo, w)
                    up(0, nxt)
                    turn_g(u)
                    up(1, nxt)
                    if q % 2 == 0:
                        turn_x((q // 2 + 1) % 2, (j + (q // 2 + 1) // 2) * 16 + 16)
                    elif last and q == 3:
                        turn_x(1, 16 * (TT // 2) + 16)
                    if q % 2 == 0:
                        pe.wait_ge(s_yacc, j * 2 + (q // 2 + 1))
                    o = down(u, q % 2 * WC, q // 2, q % 2 == 0, q % 2 == 1)
                    if q % 2:
                        o.then_inc(s_y, 1)

            with pe.Fori(0, TT // 2 - 1) as j:
                shared_pair(j, False)
            pe.wait_ge(s_route, 1)
            shared_pair(TT // 2 - 1, True)
            pe.wait_ge(s_yacc, TT + 2)

            def routed(t, k, j, nxt, turn):
                if nxt:
                    r = pe.value_load(tile_tab[0:1, 0, bass.ds(t + 1, 1)], min_val=0, max_val=(RING - 1) * WC)
                    w = pe.value_load(tile_tab[0:1, 1, bass.ds(t + 1, 1)], min_val=3, max_val=3 * E)
                    pe.wait_ge(s_xT_l, t + (TT + 2))
                    pe.wait_ge(s_silu, t + (2 * TT + 1))
                    pe.wait_ge(s_wlo, w)
                    up(0, r)
                turn_g(t + 2 * TT)
                if nxt:
                    up(1, r)
                if turn:
                    turn_x(k, (j + 1) * 16 + (16 * (TT // 2) + 16))
                r0 = pe.value_load(tile_tab[0:1, 0, bass.ds(t, 1)], min_val=0, max_val=(RING - 1) * WC)
                pe.wait_ge(s_ycp, t + 1)
                down(t + 2 * TT, r0, k, True, True).then_inc(s_y, 1)

            with pe.Fori(0, (RT - 2) // 2) as j:
                for k in range(2):
                    routed(j * 2 + k, k, j, True, True)
            for t in range((RT - 2) // 2 * 2, RT):
                routed(t, t % 2, t // 2, t + 1 < RT, t + 2 < RT)


def kernel(**inputs):
    import numpy as np
    import concourse.bacc as bacc
    from concourse.bass_utils import run_bass_kernel_spmd as run

    a = {k: np.asarray(v) for k, v in inputs.items()}

    def expert(w1, w3, w2):
        up = np.concatenate([w1.reshape(KC, P, F), w3.reshape(KC, P, F)], axis=2).transpose(1, 0, 2)
        pad = np.concatenate([w2, np.zeros((len(FCH) * P - F, D), w2.dtype)])
        return np.concatenate([up.reshape(P, W13), pad.reshape(len(FCH), P, D).transpose(1, 0, 2).reshape(P, W2C)], axis=1)

    sw1, sw3, sw2 = (a["L0_ffn_" + n].T for n in ("sw1", "sw3", "sw2"))
    parts = [expert(sw1[:, s:s + F], sw3[:, s:s + F], sw2[s:s + F]) for s in (0, F)]
    parts += [expert(a["L0_ffn_W1"][e], a["L0_ffn_W3"][e], a["L0_ffn_W2"][e]) for e in range(E)]
    arrays = {
        "x": a["x"],
        "ctxT": a["ctx_1024"].transpose(0, 2, 1),
        "wqk": np.concatenate([a["L0_xattn_Wq"], a["L0_xattn_Wk"]]).T,
        "bqk": np.stack([a["L0_xattn_bq"], a["L0_xattn_bk"]], axis=1),
        "gwT": a["L0_ffn_gate_w"].T,
        "rbias": np.broadcast_to(a["L0_ffn_router_bias"], (P, E)),
        "gates": np.broadcast_to(np.concatenate([a["g_xattn"], a["g_ffn"]]), (P, 2)),
        "wall": np.concatenate(parts, axis=1),
    }
    arrays = {k: np.ascontiguousarray(v) for k, v in arrays.items()}
    nc = bacc.Bacc("TRN2", target_bir_lowering=False, num_devices=1)
    args = [nc.dram_tensor(k, v.shape, mybir.dt.from_np(v.dtype), kind="ExternalInput").ap() for k, v in arrays.items()]
    args.append(nc.dram_tensor("out", (B, L, D), F32, kind="ExternalOutput").ap())
    args.append(nc.dram_tensor("xn_dram", (TT * P, D), F32, kind="Internal").ap())
    args.append(nc.dram_tensor("xs_dram", (RT * P, D), F32, kind="Internal").ap())
    args.append(nc.dram_tensor("ys_dram", (RT * P, D), F32, kind="Internal").ap())
    flamingo_kernel(nc, *args)
    return run(nc, [arrays], core_ids=[0]).results[0]["out"]
```

```python
from contextlib import ExitStack

import concourse.bass as bass
from concourse import mybir

P = 128
B, L, D = 4, 512, 512
C, DQ = 256, 128
E, F = 8, 352
KC = D // P
CC = C // P
TB = L // P
TT = B * TB
FCH = [128, 128, 96]
W13, W2C = KC * 2 * F, len(FCH) * D
WC = W13 + W2C
PIECES = [(0, W13 // 2), (W13 // 2, W13 // 2), (W13, W2C)]
PARTS = 8
PART = 2 * WC // PARTS
RAW = 3 * W2C
RING = 3
RT = (2 * TT * P + E * (P - 1)) // P
EPS = 1e-5

ORDER = """N0 N1 Q0 Q1 U0 L0 L1 X0 E0 U1 V0 E1 D0 X1 N2 D1 A0 W0 L2 U2 V1 E2 A1 X2 N3 D2 W1 L3 E3 U3 V2 A2 D3
X3 W2 A3 U4 V3 M0 X4 M1 W3 U5 V4 M2 X5 R0 R1 M3 W4 T0 T1 U6 V5 X6 W5 G0 G1 R2 R3 U7 V6 X7 T2 T3 W6 V7
W7 G2 G3""".split()

F32, F32R = mybir.dt.float32, mybir.dt.float32r
I32, U32 = mybir.dt.int32, mybir.dt.uint32
ALU = mybir.AluOpType
ACT = mybir.ActivationFunctionType
AX = mybir.AxisListType.X


def flamingo_kernel(nc, x, ctxT, wqk, bqk, gwT, rbias, gates, wall, out, xn_dram, xs_dram, ys_dram):
    x_t = x.rearrange("b (t p) d -> p b t d", p=P)
    out_t = out.rearrange("b (t p) d -> (b t) p d", p=P)
    xn_t = xn_dram.rearrange("(t p) d -> t p d", p=P)
    xs_t = xs_dram.rearrange("(t p) d -> t p d", p=P)
    ys_t = ys_dram.rearrange("(t p) d -> t p d", p=P)

    with ExitStack() as es:
        def sem(name):
            return es.enter_context(nc.semaphore(name))

        place = {"at": (nc.sbuf_base + 31) // 32 * 32}

        def sb(name, shape, dt, at=None):
            n = 4
            for s in shape[1:]:
                n *= s
            off = place["at"] if at is None else at
            t = nc.alloc_sbuf_tensor_at(name, shape, dt, offset=off)
            if at is None:
                place["at"] += (n + 31) // 32 * 32
            return t

        acc = sb("acc", [P, TT * D], F32)
        ident = sb("ident", [P, P], F32)
        gw_f = sb("gw_f", [P, KC * E], F32)
        gw_h = sb("gw_h", [P, KC * E], F32R)
        gw_l = sb("gw_l", [P, KC * E], F32R)
        bias_qk = sb("bias_qk", [P, 2], F32)
        rb = sb("rb", [P, E], F32)
        gate_in = sb("gate_in", [P, 2], F32)
        tg = sb("tg", [P, 2], F32)
        logits = sb("logits", [P, TT * E], F32)
        neg_half = sb("neg_half", [P, TB], F32)
        mv = sb("mv", [P, TB, 2], F32)
        ve = sb("ve", [P, TB], F32)
        rstd = sb("rstd", [P, TB], F32)
        nb = sb("nb", [P, TB], F32)
        mv2 = sb("mv2", [P, TB, 2], F32)
        ve2 = sb("ve2", [P, TB], F32)
        rstd2 = sb("rstd2", [P, TB], F32)
        nb2 = sb("nb2", [P, TB], F32)
        st = sb("st", [P, 2 * TB, 6], F32)
        nmax = sb("nmax", [P, TB], F32)
        esum = sb("esum", [P, TB], F32)
        rsum = sb("rsum", [P, TB], F32)
        iota_e = sb("iota_e", [P, E], F32)
        iota_t = sb("iota_t", [P, RT + 1], F32)
        iota_k = sb("iota_k", [P, TT], F32)
        below = sb("below", [P, E, E], F32)
        step_r = sb("step_r", [P, E], F32)
        upper_f = sb("upper_f", [P, P], F32)
        upper = sb("upper", [P, P], F32R)
        silu = sb("silu", [P, F], F32)
        g = sb("g", [P, F], F32)
        gT_h = sb("gT_h", [P, 3, P], F32R)
        gT_l = sb("gT_l", [P, 3, P], F32R)
        raw_at = place["at"]
        raw = sb("raw", [P, RAW], F32)
        ring_h_last = place["at"] + 4 * (RING - 1) * WC
        ring_h = sb("ring_h", [P, RING * WC], F32R)
        ring_l_last = place["at"] + 4 * (RING - 1) * WC
        ring_l = sb("ring_l", [P, RING * WC], F32R)
        xTs_h = sb("xTs_h", [P, TB, D], F32R)
        xTs_l = sb("xTs_l", [P, TB, D], F32R)
        arena = place["at"]

        place["at"] = ring_h_last
        ctx_h = sb("ctx_h", [P, CC, L], F32R)
        ctx_l = sb("ctx_l", [P, CC, L], F32R)
        qk_h = sb("qk_h", [P, 2, L], F32R)
        qk_l = sb("qk_l", [P, 2, L], F32R)
        assert place["at"] <= ring_h_last + 4 * WC
        place["at"] = ring_l_last
        lnxT_h = sb("lnxT_h", [P, TB, L], F32R)
        lnxT_l = sb("lnxT_l", [P, TB, L], F32R)
        assert place["at"] <= ring_l_last + 4 * WC
        place["at"] = raw_at + 4 * 2 * PART
        att = sb("att", [P, 2, L], F32)
        wqk_f = att[:, :, :].rearrange("p a b -> p (a b)")[:, 0:CC * 2 * DQ]
        wqk_h = sb("wqk_h", [P, CC, 2 * DQ], F32R)
        wqk_l = sb("wqk_l", [P, CC, 2 * DQ], F32R)
        assert place["at"] <= raw_at + 4 * RAW
        place["at"] = arena
        attT_h = sb("attT_h", [P, TB, L], F32R)
        attT_l = sb("attT_l", [P, TB, L], F32R)
        ctx_f = sb("ctx_f", [P, CC * L], F32)
        rows = sb("rows", [P, 2, D], F32)
        zero = sb("zero", [P, D], F32)
        assert place["at"] <= 229376, place["at"]

        place["at"] = arena
        xs = sb("xs", [P, 2, D], F32)
        xT_h = sb("xT_h", [P, KC, P], F32R)
        xT_l = sb("xT_l", [P, KC, P], F32R)
        xd_at = place["at"]
        xd = sb("xd", [P, 4, D], F32)
        score = sb("score", [P, TT, E], F32)
        sel = sb("sel", [P, TT, E], F32)
        top8 = sb("top8", [P, TT, 8], F32)
        idx8 = sb("idx8", [P, TT, 8], U32)
        idxf = sb("idxf", [P, TT, 2], F32)
        one_hot = [sb(f"one_hot{k}", [P, TT, E], F32) for k in range(2)]
        mask = sb("mask", [P, TT * E], F32R)
        ones = sb("ones", [P, P], F32R)
        tmp = sb("tmp", [P, TT, E], F32)
        cnt = sb("cnt", [P, TT, E], F32)
        pre = [sb(f"pre{k}", [P, TT, E], F32) for k in range(2)]
        picked = sb("picked", [P, 2, TT], F32)
        wsum = sb("wsum", [P, TT], F32)
        weight = sb("weight", [P, 2, TT], F32)
        ntile = sb("ntile", [P, E], F32)
        first = sb("first", [P, E], F32)
        first_r = sb("first_r", [P, E], F32)
        slot_f = sb("slot_f", [P, TT], F32)
        slot = sb("slot", [P, 2, TT], U32)
        passed = sb("passed", [P, RT + 1, E - 1], F32)
        tile_f = sb("tile_f", [P, 2, RT + 1], F32)
        tile_tab = sb("tile_tab", [P, 2, RT + 1], I32)
        free_tab = sb("free_tab", [P, E], I32)
        assert place["at"] <= 229376, place["at"]
        place["at"] = xd_at
        ysb = sb("ysb", [P, 2, D], F32)

        bank = [es.enter_context(nc.psum_tensor(f"bank{i}", [P, 512], F32)) for i in range(8)]

        s_const = sem("s_const")
        s_pool_c = sem("s_pool_c")
        s_zero = sem("s_zero")
        s_fill = sem("s_fill")
        s_wqk_h, s_wqk_l = sem("s_wqk_h"), sem("s_wqk_l")
        s_tanh = sem("s_tanh")
        s_x, s_ctx = sem("s_x"), sem("s_ctx")
        s_ctx_h, s_ctx_l = sem("s_ctx_h"), sem("s_ctx_l")
        s_q_ps, s_q_h, s_q_l = sem("s_q_ps"), sem("s_q_h"), sem("s_q_l")
        s_bn1, s_rstd1, s_lnx = sem("s_bn1"), sem("s_rstd1"), sem("s_lnx")
        s_lx_ps, s_lx_h, s_lx_l = sem("s_lx_ps"), sem("s_lx_h"), sem("s_lx_l")
        s_e_ps, s_max, s_exp, s_rsum, s_att = (sem(f"s_{n}") for n in ("e_ps", "max", "exp", "rsum", "att"))
        s_at_ps, s_at_h, s_at_l = sem("s_at_ps"), sem("s_at_h"), sem("s_at_l")
        s_xm_ps, s_x1 = sem("s_xm_ps"), sem("s_x1")
        s_bn2, s_rstd2, s_xn = sem("s_bn2"), sem("s_rstd2"), sem("s_xn")
        s_xn_st = [sem(f"s_xn_st{k}") for k in range(2)]
        s_xt_ps, s_xt_h, s_xt_l = sem("s_xt_ps"), sem("s_xt_h"), sem("s_xt_l")
        s_lg_ps, s_lg = sem("s_lg_ps"), sem("s_lg")
        s_dve, s_pool = sem("s_dve"), sem("s_pool")
        s_score = sem("s_score")
        s_mask, s_rank_ps, s_route, s_slot = sem("s_mask"), sem("s_rank_ps"), sem("s_route"), sem("s_slot")
        s_xd = [sem(f"s_xd{k}") for k in range(4)]
        s_sc = [sem(f"s_sc{k}") for k in range(4)]
        s_wraw = [sem(f"s_wraw{k}") for k in range(3)]
        s_whi = [sem(f"s_whi{k}") for k in range(3)]
        s_wlo, s_shared = sem("s_wlo"), sem("s_shared")
        s_xs = [sem(f"s_xs{k}") for k in range(2)]
        s_xT_ps, s_xT_h, s_xT_l = sem("s_xT_ps"), sem("s_xT_h"), sem("s_xT_l")
        s_h1, s_h3, s_silu, s_g = sem("s_h1"), sem("s_h3"), sem("s_silu"), sem("s_g")
        s_th = sem("s_th")
        s_gT_ps, s_gT_h, s_gT_l = sem("s_gT_ps"), sem("s_gT_h"), sem("s_gT_l")
        s_y, s_yacc, s_ycp = sem("s_y"), sem("s_yacc"), sem("s_ycp")
        s_yst = [sem(f"s_yst{k}") for k in range(2)]
        s_gy = [sem(f"s_gy{k}") for k in range(8)]
        s_comb = sem("s_comb")
        s_out = sem("s_out")

        b_h1, b_h3, b_gT, b_y, b_xT = bank[0], bank[1], bank[2], bank[3:5], bank[5]
        b_of = {n: bank[4 + k] for k, names in enumerate((
            "Q0 E0 E2 A2 M2 T2", "Q1 E1 A1 A3 M3 T3", "L0 A0 L3 M0 T0 G", "L1 L2 E3 M1 T1")) for n in names.split()}
        b_rank = bank[6:8]
        f = lambda ap: ap.bitcast(F32)

        def wait_alone(eng, semaphore, value):
            value = eng.to_reg(value)
            eng.wait_ge(s_pool_c, 2)
            eng.wait_ge(semaphore, value)

        block = es.enter_context(nc.Block())

        @block.sync
        def _(sp):
            ctx_t = ctxT.rearrange("b (c p) l -> p b c l", p=P)

            def load_ctx(b):
                dst = ctx_f[:, :].rearrange("p (o c l) -> p o c l", o=1, c=CC)
                sp.dma_start(dst, ctx_t[:, bass.ds(b, 1)]).then_inc(s_ctx, 16)

            def load_x(b):
                dst = acc[:, b * TB * D:(b + 1) * TB * D].rearrange("p (t d) -> p t d", t=TB)
                sp.dma_start(dst, x_t[:, b]).then_inc(s_x, 16)

            for k in range(2):
                sp.sem_inc(s_xn_st[k], 16)
            load_ctx(0)
            sp.dma_start(wqk_f.rearrange("p (c n) -> p c n", c=CC), wqk.rearrange("(c p) n -> p c n", p=P)).then_inc(s_const, 16)
            load_x(0)
            sp.dma_start(bias_qk[:, :], bqk).then_inc(s_const, 16)
            sp.dma_start(gw_f[:, :].rearrange("p (c n) -> p c n", c=KC), gwT.rearrange("(c p) n -> p c n", p=P)).then_inc(s_const, 16)
            sp.dma_start(rb[:, :], rbias).then_inc(s_const, 16)
            sp.dma_start(gate_in[:, :], gates).then_inc(s_const, 16)
            for b in range(1, B):
                sp.wait_ge(s_x, 16 * b)
                load_x(b)

            def attention_io(b, more):
                if more:
                    sp.wait_ge(s_ctx_l, b + 1)
                    load_ctx(b + 1)
                for t in range(TB):
                    sp.wait_ge(s_xn, b * TB + (t + 1))
                    sp.dma_start(xn_t[bass.ds(b * TB + t, 1)].rearrange("o p d -> p o d"),
                                 rows[:, t % 2:t % 2 + 1, :]).then_inc(s_xn_st[t % 2], 16)

            attention_io(0, True)
            sp.wait_ge(s_zero, 1)
            sp.dma_start(xs_dram.rearrange("(t p) d -> p t d", p=P),
                         zero[:, :].rearrange("p (o d) -> p o d", o=1).broadcast_to([P, RT, D])).then_inc(s_fill, 16)
            with sp.Fori(1, B - 1) as b:
                attention_io(b, True)
            attention_io(B - 1, False)

            def load_xs(t, k):
                sp.dma_start(xs[:, k:k + 1, :], xs_t[bass.ds(t, 1)].rearrange("o p d -> p o d")).then_inc(s_xs[k], 16)

            sp.wait_ge(s_xm_ps, TT)
            for k in range(2):
                sp.wait_ge(s_xn_st[k], 16 + 16 * TT // 2)
            for t in range(TT):
                k = t % 4
                if t >= 4:
                    sp.wait_ge(s_sc[k], 32 * (t // 4))
                sp.dma_start(xd[:, k, :], xn_t[t]).then_inc(s_xd[k], 16)
            for k in range(4):
                sp.wait_ge(s_sc[k], 2 * 16 * TT // 4)
            for t in range(4):
                if t >= 2:
                    sp.wait_ge(s_xT_ps, t - 1)
                load_xs(t, t % 2)

            def store_y(t, k):
                sp.wait_ge(s_ycp, t + 3)
                sp.dma_start(ys_t[bass.ds(t, 1)].rearrange("o p d -> p o d"), ysb[:, k:k + 1, :]).then_inc(s_yst[k], 16)

            with sp.Fori(0, (RT - 5) // 2) as j:
                for k in range(2):
                    sp.wait_ge(s_xT_ps, j * 2 + (k + 3))
                    load_xs(j * 2 + (k + 4), k)
                    store_y(j * 2 + k, k)
            for t in range((RT - 5) // 2 * 2, RT):
                if t + 4 < RT:
                    sp.wait_ge(s_xT_ps, t + 3)
                    load_xs(t + 4, t % 2)
                store_y(t, t % 2)
            for t in range(TT):
                sp.wait_ge(s_comb, t + 1)
                sp.dma_start(out_t[t], acc[:, t * D:(t + 1) * D]).then_inc(s_out, 16)
            sp.wait_ge(s_out, 16 * TT)

        @block.gpsimd
        def _(pool):
            gp = nc.gpsimd

            for k in range(2):
                pool.sem_inc(s_yst[k], 16)
            gp.memset(ident[:, :], 0.0).then_inc(s_pool_c, 1)
            gp.memset(zero[:, :], 0.0).then_inc(s_zero, 1)
            pool.wait_ge(s_pool_c, 1)
            gp.affine_select(out=ident[:, :], in_=ident[:, :], compare_op=ALU.not_equal, fill=1.0,
                             base=0, pattern=[[-1, P]], channel_multiplier=1).then_inc(s_pool_c, 1)
            gp.memset(neg_half[:, :], -0.5).then_inc(s_pool_c, 1)
            imprecise = dict(channel_multiplier=0, allow_small_or_imprecise_dtypes=True)
            gp.iota(iota_e[:, :], pattern=[[1, E]], base=0, **imprecise)
            gp.iota(iota_t[:, :], pattern=[[1, RT + 1]], base=0, **imprecise)
            gp.iota(iota_k[:, :], pattern=[[P, TT]], base=0, **imprecise)
            gp.memset(below[:, :, :], 1.0).then_inc(s_pool_c, 1)
            gp.memset(step_r[:, :], 1.0).then_inc(s_pool_c, 1)
            gp.memset(upper_f[:, :], 1.0).then_inc(s_pool_c, 1)
            pool.wait_ge(s_pool_c, 6)
            for e in range(1, E):
                if (e + 2) % RING == 0:
                    gp.memset(step_r[:, e - 1:e], 1.0 - RING)
            gp.affine_select(out=below[:, :, :], in_=below[:, :, :], compare_op=ALU.is_gt, fill=0.0,
                             base=0, pattern=[[1, E], [-1, E]], channel_multiplier=0)
            gp.affine_select(out=upper_f[:, :], in_=upper_f[:, :], compare_op=ALU.is_gt, fill=0.0,
                             base=0, pattern=[[1, P]], channel_multiplier=-1).then_inc(s_pool_c, 1)

            def context_lo(b):
                pool.wait_ge(s_ctx_h, b + 1)
                gp.tensor_tensor(ctx_l[:, :, :].rearrange("p c l -> p (c l)"), ctx_f[:, :],
                                 f(ctx_h[:, :, :].rearrange("p c l -> p (c l)")), ALU.subtract).then_inc(s_ctx_l, 1)

            def rstd_1(b):
                wait_alone(pool, s_bn1, b + 1)
                gp.tensor_scalar(ve[:, :], mv[:, :, 1], EPS, None, ALU.add).then_inc(s_pool, 1)
                gp.tensor_scalar(mv[:, :, 0], mv[:, :, 0], -1.0, None, ALU.mult).then_inc(s_pool, 1)
                pool.wait_ge(s_pool, b * 9 + 2)
                gp.tensor_tensor(rstd[:, :], ve[:, :], neg_half[:, :], ALU.pow).then_inc(s_pool, 1)
                pool.wait_ge(s_pool, b * 9 + 3)
                gp.tensor_tensor(nb[:, :], mv[:, :, 0], rstd[:, :], ALU.mult).then_inc(s_rstd1, 1)

            def rstd_2(b, t):
                two = slice(t, t + 2)
                wait_alone(pool, s_bn2, b * TB + (t + 2))
                gp.tensor_scalar(ve2[:, two], mv2[:, two, 1], EPS, None, ALU.add).then_inc(s_pool, 1)
                gp.tensor_scalar(mv2[:, two, 0], mv2[:, two, 0], -1.0, None, ALU.mult).then_inc(s_pool, 1)
                pool.wait_ge(s_pool, b * 9 + (5 + 3 * (t // 2)))
                gp.tensor_tensor(rstd2[:, two], ve2[:, two], neg_half[:, two], ALU.pow).then_inc(s_pool, 1)
                pool.wait_ge(s_pool, b * 9 + (6 + 3 * (t // 2)))
                gp.tensor_tensor(nb2[:, two], mv2[:, two, 0], rstd2[:, two], ALU.mult).then_inc(s_rstd2, 1)

            def load_part(i):
                if i >= 2:
                    pool.wait_ge(s_shared, i - 1)
                part = slice(i * PART, (i + 1) * PART)
                pool.dma_start(raw[:, i % 2 * PART:(i % 2 + 1) * PART], wall[:, part]).then_inc(s_wraw[i % 2], 16)
                pool.dma_start(ring_h[:, part], wall[:, part]).then_inc(s_whi[i % 2], 16)

            def split_part(i):
                part = slice(i * PART, (i + 1) * PART)
                pool.wait_ge(s_wraw[i % 2], 16 * (i // 2 + 1))
                pool.wait_ge(s_whi[i % 2], 16 * (i // 2 + 1))
                gp.tensor_tensor(ring_l[:, part], raw[:, i % 2 * PART:(i % 2 + 1) * PART], f(ring_h[:, part]),
                                 ALU.subtract).then_inc(s_shared, 1)
                if i + 2 < PARTS:
                    load_part(i + 2)

            context_lo(0)
            rstd_1(0)
            load_part(0)
            load_part(1)
            for i in range(5):
                split_part(i)
            rstd_2(0, 0)
            split_part(5)
            rstd_2(0, 2)
            split_part(6)
            split_part(7)
            with pool.Fori(1, B) as b:
                context_lo(b)
                rstd_1(b)
                rstd_2(b, 0)
                rstd_2(b, 2)

            def load_raw(e, n):
                lo, w = PIECES[n]
                pool.dma_start(raw[:, n * W2C:n * W2C + w], wall[:, bass.ds(e * WC + lo, w)]).then_inc(s_wraw[n], 16)

            pool.wait_ge(s_xm_ps, TT)
            for n in range(3):
                load_raw(2, n)
            landed = [16 * PARTS // 2, 16 * PARTS // 2, 0]

            def split_weights(e, r, k, more):
                for n, (lo, w) in enumerate(PIECES):
                    pool.dma_start(ring_h[:, bass.ds(r * WC + lo, w)], wall[:, bass.ds(e * WC + lo, w)]).then_inc(s_whi[n], 16)
                for n, (lo, w) in enumerate(PIECES):
                    pool.wait_ge(s_wraw[n], k * 16 + (landed[n] + 16))
                    pool.wait_ge(s_whi[n], k * 16 + (landed[n] + 16))
                    part = bass.ds(r * WC + lo, w)
                    gp.tensor_tensor(ring_l[:, part], raw[:, n * W2C:n * W2C + w], f(ring_h[:, part]),
                                     ALU.subtract).then_inc(s_wlo, 1)
                    if more:
                        pool.wait_ge(s_wlo, k * 3 + (n + 1))
                        load_raw(e + 1, n)

            split_weights(2, 2, 0, True)

            pool.wait_ge(s_fill, 16)
            pool.wait_ge(s_slot, 1)
            for t in range(TT):
                pool.wait_ge(s_xd[t % 4], 16 * (t // 4 + 1))
                for k in range(2):
                    pool.indirect_dma_start(xs_dram, bass.IndirectOffsetOnAxis(slot[:, k, t:t + 1], 0),
                                            xd[:, t % 4, :], None).then_inc(s_sc[t % 4], 16)

            pool.wait_ge(s_y, TT)
            split_weights(3, 0, 1, True)
            split_weights(4, 1, 2, True)
            pool.wait_ge(s_route, 1)
            for e in range(5, E + 2):
                freed = pool.value_load(free_tab[0:1, e - 2:e - 1], min_val=1, max_val=TT + RT)
                wait_alone(pool, s_y, freed)
                split_weights(e, e % RING, e - 2, e < E + 1)

            pool.wait_ge(s_wlo, 3 * E)
            pool.wait_ge(s_yst[0], 16 + 16 * ((RT + 1) // 2))
            pool.wait_ge(s_yst[1], 16 + 16 * (RT // 2))
            for t in range(TT):
                if t >= 4:
                    pool.wait_ge(s_comb, t - 3)
                for k in range(2):
                    q = 2 * (t % 4) + k
                    pool.indirect_dma_start(raw[:, q * D:(q + 1) * D], None, ys_dram,
                                            bass.IndirectOffsetOnAxis(slot[:, k, t:t + 1], 0)).then_inc(s_gy[q], 16)

        @block.scalar
        def _(act):
            a = nc.scalar
            act.wait_ge(s_const, 16 * 5)
            a.activation(wqk_h[:, :, :].rearrange("p c n -> p (c n)"), wqk_f, ACT.Copy).then_inc(s_wqk_h, 1)
            a.activation(gw_h[:, :], gw_f[:, :], ACT.Copy).then_inc(s_wqk_h, 1)
            a.activation(tg[:, :], gate_in[:, :], ACT.Tanh).then_inc(s_tanh, 1)

            def copy_hi(dst, src, ready, count, done):
                act.wait_ge(ready, count)
                a.activation(dst, src, ACT.Copy).then_inc(done, 1)

            def hidden(u):
                act.wait_ge(s_h1, u + 1)
                act.wait_ge(s_g, u + 1)
                a.activation(silu[:, :], b_h1[:, 0:F], ACT.Tanh, scale=0.5).then_inc(s_th, 1)

            def gT_hi(u):
                act.wait_ge(s_gT_ps, u + 1)
                a.activation(gT_h[:, :, :].rearrange("p c n -> p (c n)")[:, 0:2 * P], b_gT[:, 0:2 * P], ACT.Copy)
                a.activation(gT_h[0:FCH[2], 2, :], b_gT[0:FCH[2], 2 * P:3 * P], ACT.Copy).then_inc(s_gT_h, 1)

            def attention(b, shared):
                def tile(t):
                    return acc[:, bass.ds(b * TB * D + t * D, D)]

                def stage_N(t):
                    if t == 0:
                        wait_alone(act, s_rstd1, b + 1)
                    if t < 2:
                        wait_alone(act, s_xn_st[t], b * 32 + 16)
                    a.activation(rows[:, t % 2, :], tile(t), ACT.Identity, bias=nb[:, t:t + 1],
                                 scale=rstd[:, t:t + 1]).then_inc(s_lnx, 1)

                def stage_Q(k):
                    act.wait_ge(s_q_ps, b * 2 + (k + 1))
                    a.activation(qk_h[:, k, :], b_of[f"Q{k}"][:, :], ACT.Identity, bias=bias_qk[:, k:k + 1]).then_inc(s_q_h, 1)

                def stage_L(t):
                    copy_hi(lnxT_h[:, :, t * P:(t + 1) * P], b_of[f"L{t}"][:, :].rearrange("p (c l) -> p c l", c=TB),
                            s_lx_ps, b * TB + (t + 1), s_lx_h)

                def stage_E(t):
                    act.wait_ge(s_max, b * TB + (t + 1))
                    a.activation(att[:, t % 2, :], b_of[f"E{t}"][:, :], ACT.Exp, bias=nmax[:, t:t + 1],
                                 accum_out=esum[:, t:t + 1]).then_inc(s_exp, 1)

                def stage_D(t):
                    act.wait_ge(s_rsum, b * TB + (t + 1))
                    a.activation(att[:, t % 2, :], att[:, t % 2, :], ACT.Copy, scale=rsum[:, t:t + 1]).then_inc(s_att, 1)

                def stage_A(t):
                    copy_hi(attT_h[:, :, t * P:(t + 1) * P], b_of[f"A{t}"][:, :].rearrange("p (c l) -> p c l", c=TB),
                            s_at_ps, b * TB + (t + 1), s_at_h)

                def stage_R(t):
                    if t % 2 == 0:
                        wait_alone(act, s_rstd2, b * 2 + (t // 2 + 1))
                    if t >= 2:
                        wait_alone(act, s_xn_st[t % 2], b * 32 + 32)
                    a.activation(rows[:, t % 2, :], tile(t), ACT.Identity, bias=nb2[:, t:t + 1],
                                 scale=rstd2[:, t:t + 1]).then_inc(s_xn, 1)

                def stage_T(t):
                    copy_hi(xTs_h[:, t, :], b_of[f"T{t}"][:, :], s_xt_ps, b * TB + (t + 1), s_xt_h)

                stages = {"N": stage_N, "Q": stage_Q, "L": stage_L, "E": stage_E, "D": stage_D, "A": stage_A,
                          "R": stage_R, "T": stage_T}
                if shared:
                    stages |= {"U": lambda q: hidden(b * 8 + (q - 8)), "V": lambda q: gT_hi(b * 8 + (q - 8))}
                act.wait_ge(s_ctx, b * 16 + 16)
                a.activation(ctx_h[:, :, :].rearrange("p c l -> p (c l)"), ctx_f[:, :], ACT.Copy).then_inc(s_ctx_h, 1)
                for name in ORDER:
                    if name[0] in stages:
                        stages[name[0]](int(name[1]))

            act.sem_inc(s_g, 1)
            act.sem_inc(s_ycp, 2)
            attention(0, False)
            with act.Fori(1, B) as b:
                attention(b, True)

            act.wait_ge(s_lg, B)
            act.wait_ge(s_xn_st[0], 16 + 16 * TT // 2)
            act.wait_ge(s_xn_st[1], 16 + 16 * TT // 2)
            act.wait_ge(s_fill, 16)
            a.activation(score[:, :, :].rearrange("p t e -> p (t e)"), logits[:, :], ACT.Sigmoid).then_inc(s_score, 1)

            u0 = 8 * (B - 1)
            hidden(u0)
            for q in range(1, 8):
                hidden(u0 + q)
                gT_hi(u0 + q - 1)

            def hidden_silu(u):
                act.wait_ge(s_h1, u + 1)
                act.wait_ge(s_g, u + 1)
                a.activation(silu[:, :], b_h1[:, 0:F], ACT.Silu).then_inc(s_silu, 1)

            def xT_hi(n):
                act.wait_ge(s_xT_ps, n + 1)
                a.activation(xT_h[:, :, :].rearrange("p c n -> p (c n)"), b_xT[:, :], ACT.Copy).then_inc(s_xT_h, 1)

            xT_hi(0)
            hidden_silu(2 * TT)
            gT_hi(2 * TT - 1)
            xT_hi(1)

            def routed(t, k, j, nxt, turn):
                if nxt:
                    hidden_silu(t + (2 * TT + 1))
                gT_hi(t + 2 * TT)
                if turn:
                    xT_hi(t + 2)
                act.wait_ge(s_y, t + (TT + 1))
                act.wait_ge(s_yst[k], j * 16 + 16)
                a.activation(ysb[:, k, :], b_y[k][:, :], ACT.Copy).then_inc(s_ycp, 1)

            with act.Fori(0, (RT - 2) // 2) as j:
                for k in range(2):
                    routed(j * 2 + k, k, j, True, True)
            for t in range((RT - 2) // 2 * 2, RT):
                routed(t, t % 2, t // 2, t + 1 < RT, t + 2 < RT)

        @block.vector
        def _(dve):
            v = nc.vector
            chain = {"n": 0}

            def link(ins, base=0):
                chain["n"] += 1
                ins.then_inc(s_dve, 1)
                if isinstance(base, int):
                    dve.wait_ge(s_dve, base + chain["n"])
                else:
                    wait_alone(dve, s_dve, base + chain["n"])

            dve.wait_ge(s_wqk_h, 2)
            v.tensor_tensor(wqk_l[:, :, :].rearrange("p c n -> p (c n)"), wqk_f,
                            f(wqk_h[:, :, :].rearrange("p c n -> p (c n)")), ALU.subtract).then_inc(s_wqk_l, 1)
            v.tensor_tensor(gw_l[:, :], gw_f[:, :], f(gw_h[:, :]), ALU.subtract).then_inc(s_wqk_l, 1)
            dve.wait_ge(s_tanh, 1)
            per_b = 1 + TB

            def half(u):
                dve.wait_ge(s_th, u + 1)
                v.scalar_tensor_tensor(out=silu[:, :], in0=silu[:, :], scalar=1.0, in1=b_h1[:, 0:F],
                                       op0=ALU.add, op1=ALU.mult).then_inc(s_silu, 1)

            def shared_product(u):
                dve.wait_ge(s_silu, u + 2)
                dve.wait_ge(s_h3, u + 1)
                v.scalar_tensor_tensor(out=g[:, :], in0=silu[:, :], scalar=0.5, in1=b_h3[:, 0:F],
                                       op0=ALU.mult, op1=ALU.mult).then_inc(s_g, 1)

            def gT_lo(u):
                dve.wait_ge(s_gT_h, u + 1)
                v.tensor_tensor(gT_l[:, :, :].rearrange("p c n -> p (c n)")[:, 0:2 * P], b_gT[:, 0:2 * P],
                                f(gT_h[:, :, :].rearrange("p c n -> p (c n)")[:, 0:2 * P]), ALU.subtract)
                v.tensor_tensor(gT_l[0:FCH[2], 2, :], b_gT[0:FCH[2], 2 * P:3 * P], f(gT_h[0:FCH[2], 2, :]),
                                ALU.subtract).then_inc(s_gT_l, 1)

            def add_shared(n):
                tile = acc[:, bass.ds(n * D, D)]
                dve.wait_ge(s_y, n + 1)
                v.scalar_tensor_tensor(out=tile, in0=b_y[0][:, :], scalar=tg[:, 1:2], in1=tile,
                                       op0=ALU.mult, op1=ALU.add).then_inc(s_yacc, 1)

            def copy_logits(b):
                dve.wait_ge(s_lg_ps, b + 1)
                v.tensor_copy(logits[:, bass.ds(b * TB * E, TB * E)], b_of["G"][:, 0:TB * E]).then_inc(s_lg, 1)

            def sub_hi(dst, src, hi, ready, count, done):
                dve.wait_ge(ready, count)
                v.tensor_tensor(dst, src, f(hi), ALU.subtract).then_inc(done, 1)

            def attention(b, shared):
                chain["n"] = 0
                base = b * per_b

                def tile(t):
                    return acc[:, bass.ds(b * TB * D + t * D, D)]

                def cols(t):
                    return slice(t * P, (t + 1) * P)

                def stage_Q(k):
                    dve.wait_ge(s_q_h, b * 2 + (k + 1))
                    v.scalar_tensor_tensor(out=qk_l[:, k, :], in0=b_of[f"Q{k}"][:, :], scalar=bias_qk[:, k:k + 1],
                                           in1=f(qk_h[:, k, :]), op0=ALU.add, op1=ALU.subtract).then_inc(s_q_l, 1)

                def stage_L(t):
                    sub_hi(lnxT_l[:, :, cols(t)], b_of[f"L{t}"][:, :].rearrange("p (c l) -> p c l", c=TB),
                           lnxT_h[:, :, cols(t)], s_lx_h, b * TB + (t + 1), s_lx_l)

                def stage_E(t):
                    dve.wait_ge(s_e_ps, b * TB + (t + 1))
                    v.tensor_reduce(nmax[:, t:t + 1], b_of[f"E{t}"][:, :], AX, ALU.max, negate=True).then_inc(s_max, 1)

                def stage_D(t):
                    dve.wait_ge(s_exp, b * TB + (t + 1))
                    v.reciprocal(rsum[:, t:t + 1], esum[:, t:t + 1]).then_inc(s_rsum, 1)

                def stage_A(t):
                    sub_hi(attT_l[:, :, cols(t)], b_of[f"A{t}"][:, :].rearrange("p (c l) -> p c l", c=TB),
                           attT_h[:, :, cols(t)], s_at_h, b * TB + (t + 1), s_at_l)

                def stage_M(t):
                    dve.wait_ge(s_xm_ps, b * TB + (t + 1))
                    v.scalar_tensor_tensor(out=tile(t), in0=b_of[f"M{t}"][:, :], scalar=tg[:, 0:1], in1=tile(t),
                                           op0=ALU.mult, op1=ALU.add).then_inc(s_x1, 1)
                    wait_alone(dve, s_x1, b * TB + (t + 1))
                    link(v.bn_stats(st[:, TB + t, :], tile(t)), base)
                    v.bn_aggr(mv2[:, t, :], st[:, TB + t, :]).then_inc(s_bn2, 1)

                def stage_T(t):
                    sub_hi(xTs_l[:, t, :], b_of[f"T{t}"][:, :], xTs_h[:, t, :], s_xt_h, b * TB + (t + 1), s_xt_l)

                stages = {"Q": stage_Q, "L": stage_L, "E": stage_E, "D": stage_D, "A": stage_A, "M": stage_M, "T": stage_T}
                if shared:
                    stages |= {"U": lambda q: half(b * 8 + (q - 8)), "X": lambda q: shared_product(b * 8 + (q - 8)),
                               "V": lambda q: gT_lo(b * 8 + (q - 8)),
                               "W": lambda q: add_shared(b * TB + (q // 2 - TB)) if q % 2 else None}
                wait_alone(dve, s_x, b * 16 + 16)
                for t in range(TB):
                    o = v.bn_stats(st[:, t, :], tile(t))
                link(o, base)
                for t in range(TB):
                    o = v.bn_aggr(mv[:, t, :], st[:, t, :])
                o.then_inc(s_bn1, 1)
                if shared:
                    copy_logits(b - 1)
                for name in ORDER:
                    if name[0] in stages:
                        stages[name[0]](int(name[1]))

            dve.sem_inc(s_silu, 1)
            dve.sem_inc(s_yacc, 1)
            attention(0, False)
            with dve.Fori(1, B) as b:
                attention(b, True)
            copy_logits(B - 1)

            u0 = 8 * (B - 1)
            half(u0)
            base = B * per_b
            chain["n"] = 0

            def over(ap, n):
                return ap.rearrange("p (o k) -> p o k", o=1).broadcast_to([P, n, ap.shape[1]])

            dve.wait_ge(s_score, 1)
            dve.wait_ge(s_pool_c, 7)
            link(v.tensor_tensor(sel[:, :, :], score[:, :, :], over(rb[:, :], TT), ALU.add), base)
            for t in range(TT):
                o = v.max(top8[:, t, :], sel[:, t, :])
            link(o, base)
            for t in range(TT):
                o = v.max_index(idx8[:, t, :], top8[:, t, :], sel[:, t, :])
            link(o, base)
            link(v.tensor_copy(idxf[:, :, :], idx8[:, :, 0:2]), base)
            ie = over(iota_e[:, :], TT)
            for k in range(2):
                o = v.tensor_tensor(one_hot[k][:, :, :], ie, idxf[:, :, k:k + 1].broadcast_to([P, TT, E]), ALU.is_equal)
            link(o, base)
            v.tensor_copy(upper[:, :], upper_f[:, :])
            v.memset(f(ones[:, :]), 1.0)
            v.tensor_tensor(mask[:, :].rearrange("p (t e) -> p t e", t=TT), one_hot[0][:, :, :], one_hot[1][:, :, :], ALU.add).then_inc(s_mask, 1)
            shared_product(u0)

            def shared_step(q):
                half(u0 + q)
                gT_lo(u0 + q - 1)
                shared_product(u0 + q)
                if q % 2 == 0:
                    add_shared(TT - TB + q // 2 - 1)

            shared_step(1)
            for k in range(2):
                link(v.tensor_tensor(tmp[:, :, :], one_hot[k][:, :, :], score[:, :, :], ALU.mult), base)
                link(v.tensor_reduce(picked[:, k, :], tmp[:, :, :], AX, ALU.add), base)
            link(v.tensor_tensor(wsum[:, :], picked[:, 0, :], picked[:, 1, :], ALU.add), base)
            link(v.tensor_scalar(wsum[:, :], wsum[:, :], 1e-12, None, ALU.max), base)
            link(v.reciprocal(wsum[:, :], wsum[:, :]), base)
            for k in range(2):
                link(v.tensor_tensor(picked[:, k, :], picked[:, k, :], wsum[:, :], ALU.mult), base)
                link(v.tensor_scalar(weight[:, k, :], picked[:, k, :], tg[:, 1:2], None, ALU.mult), base)
            shared_step(2)
            dve.wait_ge(s_rank_ps, 1)
            v.tensor_copy(cnt[:, :, :].rearrange("p t e -> p (t e)"), b_rank[1][:, 0:TT * E])
            link(v.tensor_copy(pre[0][:, :, :].rearrange("p t e -> p (t e)"), b_rank[1][:, 0:TT * E]), base)
            s, k = 1, 0
            while s < TT:
                v.tensor_copy(pre[1 - k][:, 0:s, :], pre[k][:, 0:s, :])
                link(v.tensor_tensor(pre[1 - k][:, s:, :], pre[k][:, s:, :], pre[k][:, 0:TT - s, :], ALU.add), base)
                s, k = 2 * s, 1 - k
            incl = pre[k]
            total = incl[:, TT - 1:TT, :].rearrange("p o e -> p e o")
            cmp = tmp[:, :, :].rearrange("p t e -> p (t e)").rearrange("p (e t) -> p e t", e=E)
            link(v.tensor_tensor(cmp, total.broadcast_to([P, E, TT]), over(iota_k[:, :], E), ALU.is_gt), base)
            link(v.tensor_reduce(ntile[:, :], cmp, AX, ALU.add), base)
            less = tmp[:, 0:E, :]
            link(v.tensor_tensor(less, below[:, :, :], over(ntile[:, :], E), ALU.mult), base)
            link(v.tensor_reduce(first[:, :], less, AX, ALU.add), base)
            link(v.tensor_scalar(first_r[:, :], first[:, :], float(P), None, ALU.mult), base)
            link(v.tensor_tensor(cnt[:, :, :], incl[:, :, :], cnt[:, :, :], ALU.subtract), base)
            link(v.tensor_tensor(cnt[:, :, :], cnt[:, :, :], over(first_r[:, :], TT), ALU.add), base)
            link(v.tensor_tensor(cnt[:, :, :].rearrange("p t e -> p (t e)"), b_rank[0][:, 0:TT * E],
                                 cnt[:, :, :].rearrange("p t e -> p (t e)"), ALU.add), base)
            for k in range(2):
                link(v.tensor_tensor(tmp[:, :, :], one_hot[k][:, :, :], cnt[:, :, :], ALU.mult), base)
                link(v.tensor_reduce(slot_f[:, :], tmp[:, :, :], AX, ALU.add), base)
                link(v.tensor_copy(slot[:, k, :], slot_f[:, :]), base)
            dve.sem_inc(s_slot, 1)
            shared_step(3)
            fe = over(first[:, 1:E], RT + 1)
            link(v.tensor_tensor(passed[:, :, :], iota_t[:, :].rearrange("p (t o) -> p t o", o=1).broadcast_to([P, RT + 1, E - 1]), fe, ALU.is_ge), base)
            link(v.tensor_reduce(tile_f[:, 1, :], passed[:, :, :], AX, ALU.add), base)
            link(v.tensor_tensor(passed[:, :, :], passed[:, :, :],
                                 over(step_r[:, 0:E - 1], RT + 1), ALU.mult), base)
            link(v.tensor_reduce(tile_f[:, 0, :], passed[:, :, :], AX, ALU.add), base)
            link(v.tensor_scalar(tile_f[:, 0, :], tile_f[:, 0, :], float(WC), 2.0 * WC, ALU.mult, ALU.add), base)
            link(v.tensor_scalar(tile_f[:, 1, :], tile_f[:, 1, :], 3.0, 3.0, ALU.mult, ALU.add), base)
            link(v.tensor_copy(tile_tab[:, :, :], tile_f[:, :, :]), base)
            link(v.tensor_scalar(first_r[:, :], first[:, :], float(TT), None, ALU.add), base)
            v.tensor_copy(free_tab[:, 2:E], first_r[:, 0:E - 2])
            link(v.tensor_copy(free_tab[:, 0:2], first_r[:, 0:2]), base)
            dve.sem_inc(s_route, 1)

            for q in range(4, 8):
                shared_step(q)

            def xT_lo(n):
                dve.wait_ge(s_xT_h, n + 1)
                v.tensor_tensor(xT_l[:, :, :].rearrange("p c n -> p (c n)"), b_xT[:, :],
                                f(xT_h[:, :, :].rearrange("p c n -> p (c n)")), ALU.subtract).then_inc(s_xT_l, 1)

            def product(u):
                dve.wait_ge(s_silu, u + 2)
                dve.wait_ge(s_h3, u + 1)
                v.tensor_tensor(g[:, :], silu[:, :], b_h3[:, 0:F], ALU.mult).then_inc(s_g, 1)

            xT_lo(0)
            gT_lo(2 * TT - 1)
            product(2 * TT)
            xT_lo(1)
            add_shared(TT - 1)

            def routed(t, nxt, turn):
                gT_lo(t + 2 * TT)
                if nxt:
                    product(t + (2 * TT + 1))
                if turn:
                    xT_lo(t + 2)

            with dve.Fori(0, (RT - 2) // 2) as j:
                for k in range(2):
                    routed(j * 2 + k, True, True)
            for t in range((RT - 2) // 2 * 2, RT):
                routed(t, t + 1 < RT, t + 2 < RT)

            for t in range(TT):
                tile = acc[:, t * D:(t + 1) * D]
                for k in range(2):
                    q = 2 * (t % 4) + k
                    dve.wait_ge(s_gy[q], 16 * (t // 4 + 1))
                    o = v.scalar_tensor_tensor(out=tile, in0=raw[:, q * D:(q + 1) * D], scalar=weight[:, k, t:t + 1], in1=tile,
                                               op0=ALU.mult, op1=ALU.add)
                    if k == 0:
                        link(o, base)
                o.then_inc(s_comb, 1)

        @block.tensor
        def _(pe):
            t_ = nc.tensor

            def product3(out, pairs):
                n = 0
                for sh, sl, mh, ml in pairs:
                    for s, m in ((sh, mh), (sh, ml), (sl, mh)):
                        o = t_.matmul(out, s, m, start=(n == 0), stop=(n == 3 * len(pairs) - 1))
                        n += 1
                return o


            def turn(dst, src, s):
                for c in range(4):
                    o = t_.transpose(dst[:, c * P:(c + 1) * P], src[:, c * P:(c + 1) * P], ident[:, :])
                o.then_inc(s, 1)

            def up(which, r, xh, xl):
                pairs = []
                for c in range(KC):
                    lo = c * 2 * F + which * F
                    pairs.append((xh[:, c * P:(c + 1) * P], xl[:, c * P:(c + 1) * P],
                                  ring_h[:, bass.ds(r + lo, F)], ring_l[:, bass.ds(r + lo, F)]))
                product3((b_h1, b_h3)[which][:, 0:F], pairs).then_inc((s_h1, s_h3)[which], 1)

            def turn_g(u):
                pe.wait_ge(s_g, u + 2)
                for c, w in enumerate(FCH):
                    o = t_.transpose(b_gT[0:w, c * P:(c + 1) * P], g[:, c * P:c * P + w], ident[:, :])
                o.then_inc(s_gT_ps, 1)

            def down(u, r, k, start, stop):
                pe.wait_ge(s_gT_l, u + 1)
                n, last = 0, 3 * len(FCH) - 1
                for c, w in enumerate(FCH):
                    lo = W13 + c * D
                    mh, ml = ring_h[0:w, bass.ds(r + lo, D)], ring_l[0:w, bass.ds(r + lo, D)]
                    for s, m in ((gT_h[0:w, c, :], mh), (gT_h[0:w, c, :], ml), (gT_l[0:w, c, :], mh)):
                        o = t_.matmul(b_y[k][:, :], s, m, start=(start and n == 0), stop=(stop and n == last))
                        n += 1
                return o

            def shared_up(u, q, which):
                if which == 0:
                    pe.wait_ge(s_silu, u + 1)
                up(which, q % 2 * WC, xTs_h[:, q // 2, :], xTs_l[:, q // 2, :])

            def shared_down(u, q, n):
                if q % 2 == 0:
                    pe.wait_ge(s_yacc, n + 1)
                o = down(u, q % 2 * WC, 0, q % 2 == 0, q % 2 == 1)
                if q % 2:
                    o.then_inc(s_y, 1)

            def attention(b, shared):
                def stage_Q(k):
                    if k == 0:
                        pe.wait_ge(s_ctx_l, b + 1)
                    cols = slice(k * DQ, (k + 1) * DQ)
                    product3(b_of[f"Q{k}"][:, :], [(wqk_h[:, c, cols], wqk_l[:, c, cols], ctx_h[:, c, :], ctx_l[:, c, :])
                                                   for c in range(CC)]).then_inc(s_q_ps, 1)

                def stage_L(t):
                    pe.wait_ge(s_lnx, b * TB + (t + 1))
                    if t == 0 and shared:
                        pe.wait_ge(s_lg, b)
                    if t == 2:
                        pe.wait_ge(s_lx_l, b * TB + 2)
                    if t == 3:
                        pe.wait_ge(s_at_l, b * TB + 1)
                    turn(b_of[f"L{t}"], rows[:, t % 2, :], s_lx_ps)

                def stage_E(t):
                    if t == 0:
                        pe.wait_ge(s_q_l, b * 2 + 2)
                    if t == 3:
                        pe.wait_ge(s_lx_l, b * TB + 3)
                    rs = slice(t * P, (t + 1) * P)
                    product3(b_of[f"E{t}"][:, :], [(qk_h[:, 0, rs], qk_l[:, 0, rs], qk_h[:, 1, :], qk_l[:, 1, :])]).then_inc(s_e_ps, 1)

                def stage_A(t):
                    pe.wait_ge(s_att, b * TB + (t + 1))
                    if t == 0:
                        pe.wait_ge(s_lx_l, b * TB + 1)
                    if t == 3:
                        pe.wait_ge(s_at_l, b * TB + 2)
                    turn(b_of[f"A{t}"], att[:, t % 2, :], s_at_ps)

                def stage_M(t):
                    if t == 0:
                        pe.wait_ge(s_lx_l, b * TB + TB)
                        pe.wait_ge(s_at_l, b * TB + TB)
                    rs = slice(t * P, (t + 1) * P)
                    product3(b_of[f"M{t}"][:, :], [(lnxT_h[:, c, rs], lnxT_l[:, c, rs], attT_h[:, c, :], attT_l[:, c, :])
                                                   for c in range(TB)]).then_inc(s_xm_ps, 1)

                def stage_T(t):
                    pe.wait_ge(s_xn, b * TB + (t + 1))
                    turn(b_of[f"T{t}"], rows[:, t % 2, :], s_xt_ps)

                def stage_G(t):
                    pe.wait_ge(s_xt_l, b * TB + (t + 1))
                    o = product3(b_of["G"][:, t * E:(t + 1) * E],
                                 [(xTs_h[:, t, c * P:(c + 1) * P], xTs_l[:, t, c * P:(c + 1) * P],
                                   gw_h[:, c * E:(c + 1) * E], gw_l[:, c * E:(c + 1) * E]) for c in range(KC)])
                    if t == TB - 1:
                        o.then_inc(s_lg_ps, 1)

                stages = {"Q": stage_Q, "L": stage_L, "E": stage_E, "A": stage_A, "M": stage_M, "T": stage_T, "G": stage_G}
                if shared:
                    stages |= {"U": lambda q: shared_up(b * 8 + (q - 8), q, 0), "X": lambda q: shared_up(b * 8 + (q - 8), q, 1),
                               "V": lambda q: turn_g(b * 8 + (q - 8)),
                               "W": lambda q: shared_down(b * 8 + (q - 8), q, b * TB + (q // 2 - TB))}
                for name in ORDER:
                    if name[0] in stages:
                        stages[name[0]](int(name[1]))

            pe.wait_ge(s_wqk_l, 2)
            pe.wait_ge(s_pool_c, 3)
            attention(0, False)
            pe.wait_ge(s_shared, PARTS)
            with pe.Fori(1, B) as b:
                attention(b, True)

            u0 = 8 * (B - 1)
            shared_up(u0, 0, 0)
            shared_up(u0, 0, 1)
            for q in range(1, 8):
                shared_up(u0 + q, q, 0)
                if q == 1:
                    pe.wait_ge(s_mask, 1)
                    t_.matmul(b_rank[0][:, 0:TT * E], upper[:, :], mask[:, :], start=True, stop=True)
                    t_.matmul(b_rank[1][:, 0:TT * E], ones[:, :], mask[:, :], start=True, stop=True).then_inc(s_rank_ps, 1)
                turn_g(u0 + q - 1)
                shared_up(u0 + q, q, 1)
                shared_down(u0 + q - 1, q - 1, TT - TB + (q - 1) // 2)

            def turn_x(k, landed):
                pe.wait_ge(s_xs[k], landed)
                for c in range(KC):
                    o = t_.transpose(b_xT[:, c * P:(c + 1) * P], xs[:, k, c * P:(c + 1) * P], ident[:, :])
                o.then_inc(s_xT_ps, 1)

            turn_x(0, 16)
            r = pe.value_load(tile_tab[0:1, 0, 0:1], min_val=0, max_val=(RING - 1) * WC)
            w = pe.value_load(tile_tab[0:1, 1, 0:1], min_val=3, max_val=3 * E)
            xh, xl = (x[:, :, :].rearrange("p c n -> p (c n)") for x in (xT_h, xT_l))
            pe.wait_ge(s_xT_l, 1)
            pe.wait_ge(s_silu, 2 * TT + 1)
            pe.wait_ge(s_wlo, w)
            up(0, r, xh, xl)
            turn_g(2 * TT - 1)
            up(1, r, xh, xl)
            turn_x(1, 16)
            shared_down(2 * TT - 1, 7, TT - 1)
            pe.wait_ge(s_yacc, TT + 1)

            def routed(t, k, j, nxt, turn):
                if nxt:
                    r = pe.value_load(tile_tab[0:1, 0, bass.ds(t + 1, 1)], min_val=0, max_val=(RING - 1) * WC)
                    w = pe.value_load(tile_tab[0:1, 1, bass.ds(t + 1, 1)], min_val=3, max_val=3 * E)
                    pe.wait_ge(s_xT_l, t + 2)
                    pe.wait_ge(s_silu, t + (2 * TT + 2))
                    pe.wait_ge(s_wlo, w)
                    up(0, r, xh, xl)
                turn_g(t + 2 * TT)
                if nxt:
                    up(1, r, xh, xl)
                if turn:
                    turn_x(k, j * 16 + 32)
                r0 = pe.value_load(tile_tab[0:1, 0, bass.ds(t, 1)], min_val=0, max_val=(RING - 1) * WC)
                pe.wait_ge(s_ycp, t + 1)
                down(t + 2 * TT, r0, k, True, True).then_inc(s_y, 1)

            with pe.Fori(0, (RT - 2) // 2) as j:
                for k in range(2):
                    routed(j * 2 + k, k, j, True, True)
            for t in range((RT - 2) // 2 * 2, RT):
                routed(t, t % 2, t // 2, t + 1 < RT, t + 2 < RT)


def kernel(**inputs):
    import numpy as np
    import concourse.bacc as bacc
    from concourse.bass_utils import run_bass_kernel_spmd as run

    a = {k: np.asarray(v) for k, v in inputs.items()}

    def expert(w1, w3, w2):
        up = np.concatenate([w1.reshape(KC, P, F), w3.reshape(KC, P, F)], axis=2).transpose(1, 0, 2)
        pad = np.concatenate([w2, np.zeros((len(FCH) * P - F, D), w2.dtype)])
        return np.concatenate([up.reshape(P, W13), pad.reshape(len(FCH), P, D).transpose(1, 0, 2).reshape(P, W2C)], axis=1)

    sw1, sw3, sw2 = (a["L0_ffn_" + n].T for n in ("sw1", "sw3", "sw2"))
    parts = [expert(sw1[:, s:s + F], sw3[:, s:s + F], sw2[s:s + F]) for s in (0, F)]
    parts += [expert(a["L0_ffn_W1"][e], a["L0_ffn_W3"][e], a["L0_ffn_W2"][e]) for e in range(E)]
    arrays = {
        "x": a["x"],
        "ctxT": a["ctx_1024"].transpose(0, 2, 1),
        "wqk": np.concatenate([a["L0_xattn_Wq"], a["L0_xattn_Wk"]]).T,
        "bqk": np.stack([a["L0_xattn_bq"], a["L0_xattn_bk"]], axis=1),
        "gwT": a["L0_ffn_gate_w"].T,
        "rbias": np.broadcast_to(a["L0_ffn_router_bias"], (P, E)),
        "gates": np.broadcast_to(np.concatenate([a["g_xattn"], a["g_ffn"]]), (P, 2)),
        "wall": np.concatenate(parts, axis=1),
    }
    arrays = {k: np.ascontiguousarray(v) for k, v in arrays.items()}
    nc = bacc.Bacc("TRN2", target_bir_lowering=False, num_devices=1)
    args = [nc.dram_tensor(k, v.shape, mybir.dt.from_np(v.dtype), kind="ExternalInput").ap() for k, v in arrays.items()]
    args.append(nc.dram_tensor("out", (B, L, D), F32, kind="ExternalOutput").ap())
    args.append(nc.dram_tensor("xn_dram", (TT * P, D), F32, kind="Internal").ap())
    args.append(nc.dram_tensor("xs_dram", (RT * P, D), F32, kind="Internal").ap())
    args.append(nc.dram_tensor("ys_dram", (RT * P, D), F32, kind="Internal").ap())
    flamingo_kernel(nc, *args)
    return run(nc, [arrays], core_ids=[0]).results[0]["out"]
```

```python
from contextlib import ExitStack

import concourse.bass as bass
from concourse import mybir

P = 128
B, L, D = 4, 512, 512
C, DQ = 256, 128
E, F = 8, 352
KC = D // P
CC = C // P
TB = L // P
TT = B * TB
FCH = [128, 128, 96]
UP = 2 * F + E
W13, W2C = KC * UP, len(FCH) * D
WC = W13 + W2C
PIECES = [(0, W13 // 2), (W13 // 2, W13 // 2), (W13, W2C)]
PARTS = 8
PART = 2 * WC // PARTS
RAW = 3 * W2C
RING = 3
TAG = 1 + E
XW = D + TAG
RT = (2 * TT * P + E * (P - 1)) // P
LT = 2 * TT // 4 * 4
EPS = 1e-5

ORDER = """N0 N1 Q0 Q1 U0 L0 L1 X0 E0 U1 V0 E1 D0 X1 N2 D1 A0 W0 L2 U2 V1 E2 A1 X2 N3 D2 W1 L3 E3 U3 V2 A2 D3
X3 W2 A3 C0 U4 V3 M0 X4 M1 W3 U5 V4 M2 X5 R0 R1 M3 W4 T0 T1 U6 V5 X6 W5 R2 R3 U7 V6 X7 T2 W6 V7 T3
W7""".split()

Y0 = TT + TB
YACC = Y0 + 1

F32, F32R = mybir.dt.float32, mybir.dt.float32r
I32, U32 = mybir.dt.int32, mybir.dt.uint32
ALU = mybir.AluOpType
ACT = mybir.ActivationFunctionType
AX = mybir.AxisListType.X


def flamingo_kernel(nc, x, ctxT, wqk, bqk, rbias, gates, wall, out, xn_dram, xs_dram):
    x_t = x.rearrange("b (t p) d -> p b t d", p=P)
    out_b = out[0:TT * P].rearrange("(b t p) d -> p b t d", p=P, t=TB)
    xn_t = xn_dram.rearrange("(t p) d -> t p d", p=P)
    xs_t = xs_dram.rearrange("(t p) d -> t p d", p=P)

    with ExitStack() as es:
        def sem(name):
            return es.enter_context(nc.semaphore(name))

        place = {"at": (nc.sbuf_base + 31) // 32 * 32}

        def sb(name, shape, dt, at=None):
            n = 4
            for s in shape[1:]:
                n *= s
            off = place["at"] if at is None else at
            t = nc.alloc_sbuf_tensor_at(name, shape, dt, offset=off)
            if at is None:
                place["at"] += (n + 31) // 32 * 32
            return t

        acc = sb("acc", [P, TT * D], F32)
        ident = sb("ident", [P, P], F32)
        bias_qk = sb("bias_qk", [P, 2], F32)
        rb = sb("rb", [P, E], F32)
        gate_in = sb("gate_in", [P, 2], F32)
        tg = sb("tg", [P, 2], F32)
        logits = sb("logits", [P, TT * E], F32)
        neg_half = sb("neg_half", [P, TB], F32)
        mv = sb("mv", [P, TB, 2], F32)
        ve = sb("ve", [P, TB], F32)
        rstd = sb("rstd", [P, TB], F32)
        nb = sb("nb", [P, TB], F32)
        mv2 = sb("mv2", [P, TB, 2], F32)
        ve2 = sb("ve2", [P, TB], F32)
        rstd2 = sb("rstd2", [P, TB], F32)
        nb2 = sb("nb2", [P, TB], F32)
        st = sb("st", [P, 2 * TB, 6], F32)
        nmax = sb("nmax", [P, TB], F32)
        esum = sb("esum", [P, TB], F32)
        rsum = sb("rsum", [P, TB], F32)
        iota_e = sb("iota_e", [P, E], F32)
        iota_t = sb("iota_t", [P, RT + 1], F32)
        iota_k = sb("iota_k", [P, TT], F32)
        below = sb("below", [P, E, E], F32)
        step_r = sb("step_r", [P, E], F32)
        upper_f = sb("upper_f", [P, P], F32)
        upper = sb("upper", [P, P], F32R)
        tags = sb("tags", [P, TT, TAG], F32)
        tag = sb("tag", [P, 4, TAG], F32)
        silu = sb("silu", [P, F], F32)
        g = sb("g", [P, F], F32)
        gT_h = sb("gT_h", [P, 3, P], F32R)
        gT_l = sb("gT_l", [P, 3, P], F32R)
        raw_at = place["at"]
        raw = sb("raw", [P, RAW], F32)
        ring_h_last = place["at"] + 4 * (RING - 1) * WC
        ring_h = sb("ring_h", [P, RING * WC], F32R)
        ring_l_last = place["at"] + 4 * (RING - 1) * WC
        ring_l = sb("ring_l", [P, RING * WC], F32R)
        xTs_h = sb("xTs_h", [P, TB, D], F32R)
        xTs_l = sb("xTs_l", [P, TB, D], F32R)
        arena = place["at"]

        place["at"] = ring_h_last
        ctx_h = sb("ctx_h", [P, CC, L], F32R)
        ctx_l = sb("ctx_l", [P, CC, L], F32R)
        qk_h = sb("qk_h", [P, 2, L], F32R)
        qk_l = sb("qk_l", [P, 2, L], F32R)
        assert place["at"] <= ring_h_last + 4 * WC
        place["at"] = ring_l_last
        lnxT_h = sb("lnxT_h", [P, TB, L], F32R)
        lnxT_l = sb("lnxT_l", [P, TB, L], F32R)
        assert place["at"] <= ring_l_last + 4 * WC
        place["at"] = raw_at + 4 * 2 * PART
        att = sb("att", [P, 2, L], F32)
        wqk_f = att[:, :, :].rearrange("p a b -> p (a b)")[:, 0:CC * 2 * DQ]
        wqk_h = sb("wqk_h", [P, CC, 2 * DQ], F32R)
        wqk_l = sb("wqk_l", [P, CC, 2 * DQ], F32R)
        assert place["at"] <= raw_at + 4 * RAW
        place["at"] = arena
        attT_h = sb("attT_h", [P, TB, L], F32R)
        attT_l = sb("attT_l", [P, TB, L], F32R)
        ctx_f = sb("ctx_f", [P, CC * L], F32)
        rows = sb("rows", [P, 2, D], F32)
        blank = sb("blank", [P, XW], F32)
        assert place["at"] <= 229376, place["at"]

        place["at"] = arena
        xs = sb("xs", [P, 2, D], F32)
        xT_h = sb("xT_h", [P, KC, P], F32R)
        xT_l = sb("xT_l", [P, KC, P], F32R)
        xd_at = place["at"]
        xd = sb("xd", [P, 4, XW], F32)
        score = sb("score", [P, TT, E], F32)
        sel = sb("sel", [P, TT, E], F32)
        top8 = sb("top8", [P, TT, 8], F32)
        idx8 = sb("idx8", [P, TT, 8], U32)
        idxf = sb("idxf", [P, TT, 2], F32)
        one_hot = [sb(f"one_hot{k}", [P, TT, E], F32) for k in range(2)]
        mask = sb("mask", [P, TT * E], F32R)
        ones = sb("ones", [P, P], F32R)
        tmp = sb("tmp", [P, TT, E], F32)
        cnt = sb("cnt", [P, TT, E], F32)
        pre = [sb(f"pre{k}", [P, TT, E], F32) for k in range(2)]
        wsum = sb("wsum", [P, TT], F32)
        ntile = sb("ntile", [P, E], F32)
        first = sb("first", [P, E], F32)
        first_r = sb("first_r", [P, E], F32)
        slot_f = sb("slot_f", [P, TT], F32)
        slot = sb("slot", [P, 2, TT], U32)
        passed = sb("passed", [P, RT + 1, E - 1], F32)
        tile_f = sb("tile_f", [P, 4, RT + 1], F32)
        tile_tab = sb("tile_tab", [P, 3, RT + 1], I32)
        IN_RING, SPLIT, COLUMN = range(3)
        used = sb("used", [P, 1], I32)
        load_tab = sb("load_tab", [P, 3, RT + 2], I32)
        LOAD, INTO, FOLLOWING = range(3)
        assert place["at"] <= 229376, place["at"]
        place["at"] = xd_at
        ysb = sb("ysb", [P, 2, D], F32)

        bank = [es.enter_context(nc.psum_tensor(f"bank{i}", [P, 512], F32)) for i in range(8)]

        s_const, s_wqk = sem("s_const"), sem("s_wqk")
        s_pool_c = sem("s_pool_c")
        s_zero = sem("s_zero")
        s_fill = sem("s_fill")
        s_wqk_h, s_wqk_l = sem("s_wqk_h"), sem("s_wqk_l")
        s_tanh = sem("s_tanh")
        s_x, s_ctx = sem("s_x"), sem("s_ctx")
        s_ctx_h, s_ctx_l = sem("s_ctx_h"), sem("s_ctx_l")
        s_q_ps, s_q_h, s_q_l = sem("s_q_ps"), sem("s_q_h"), sem("s_q_l")
        s_bn1, s_rstd1, s_lnx = sem("s_bn1"), sem("s_rstd1"), sem("s_lnx")
        s_lx_ps, s_lx_h, s_lx_l = sem("s_lx_ps"), sem("s_lx_h"), sem("s_lx_l")
        s_e_ps, s_max, s_exp, s_rsum, s_att = (sem(f"s_{n}") for n in ("e_ps", "max", "exp", "rsum", "att"))
        s_at_ps, s_at_h, s_at_l = sem("s_at_ps"), sem("s_at_h"), sem("s_at_l")
        s_xm_ps, s_x1 = sem("s_xm_ps"), sem("s_x1")
        s_bn2, s_rstd2, s_xn = sem("s_bn2"), sem("s_rstd2"), sem("s_xn")
        s_xn_st = [sem(f"s_xn_st{k}") for k in range(2)]
        s_xt_ps, s_xt_h, s_xt_l = sem("s_xt_ps"), sem("s_xt_h"), sem("s_xt_l")
        s_lg_ps, s_lg = sem("s_lg_ps"), sem("s_lg")
        s_dve, s_pool, s_pool_1, s_st = sem("s_dve"), sem("s_pool"), sem("s_pool_1"), sem("s_st")
        s_score, s_tags = sem("s_score"), sem("s_tags")
        s_mask, s_rank_ps, s_route, s_slot = sem("s_mask"), sem("s_rank_ps"), sem("s_route"), sem("s_slot")
        s_xd = [sem(f"s_xd{k}") for k in range(4)]
        s_sc = [sem(f"s_sc{k}") for k in range(4)]
        s_wraw = [sem(f"s_wraw{k}") for k in range(3)]
        s_whi = [sem(f"s_whi{k}") for k in range(3)]
        s_sraw = [sem(f"s_sraw{k}") for k in range(2)]
        s_shi = [sem(f"s_shi{k}") for k in range(4)]
        s_wlo, s_shared = sem("s_wlo"), sem("s_shared")
        s_xs = [sem(f"s_xs{k}") for k in range(2)]
        s_xT_ps, s_xT_h, s_xT_l = sem("s_xT_ps"), sem("s_xT_h"), sem("s_xT_l")
        s_h1, s_h3, s_silu, s_g = sem("s_h1"), sem("s_h3"), sem("s_silu"), sem("s_g")
        s_th = sem("s_th")
        s_gT_ps, s_gT_h, s_gT_l = sem("s_gT_ps"), sem("s_gT_h"), sem("s_gT_l")
        s_y, s_yacc, s_ycp = sem("s_y"), sem("s_yacc"), sem("s_ycp")
        s_tag_in = [sem(f"s_tag_in{k}") for k in range(4)]
        s_out, s_added = sem("s_out"), sem("s_added")

        b_h1, b_h3, b_gT, b_y, b_xT = bank[0], bank[1], bank[2], bank[3:5], bank[5]
        b_of = {n: bank[4 + k] for k, names in enumerate((
            "Q0 E0 E2 A2 M2 T2", "Q1 E1 A1 A3 M3 T3", "L0 A0 L3 M0 T0 G", "L1 L2 E3 M1 T1")) for n in names.split()}
        b_rank = bank[6:8]
        f = lambda ap: ap.bitcast(F32)

        def wait_alone(eng, semaphore, value):
            value = eng.to_reg(value)
            eng.wait_ge(s_pool_c, 2)
            eng.wait_ge(semaphore, value)

        block = es.enter_context(nc.Block())

        @block.sync
        def _(sp):
            ctx_t = ctxT.rearrange("b (c p) l -> p b c l", p=P)

            def load_ctx(b):
                dst = ctx_f[:, :].rearrange("p (o c l) -> p o c l", o=1, c=CC)
                sp.dma_start(dst, ctx_t[:, bass.ds(b, 1)]).then_inc(s_ctx, 16)

            def load_x(b):
                dst = acc[:, b * TB * D:(b + 1) * TB * D].rearrange("p (t d) -> p t d", t=TB)
                sp.dma_start(dst, x_t[:, b]).then_inc(s_x, 16)

            for k in range(2):
                sp.sem_inc(s_xn_st[k], 16)

            def store_x2(b, added):
                sp.wait_ge(s_yacc, added)
                sp.dma_start(out_b[:, bass.ds(b, 1)],
                             acc[:, bass.ds(b * TB * D, TB * D)].rearrange("p (o t d) -> p o t d", o=1, t=TB)).then_inc(s_out, 16)

            load_ctx(0)
            sp.dma_start(wqk_f.rearrange("p (c n) -> p c n", c=CC), wqk.rearrange("(c p) n -> p c n", p=P)).then_inc(s_wqk, 16)
            load_x(0)
            sp.dma_start(bias_qk[:, :], bqk).then_inc(s_const, 16)
            sp.dma_start(rb[:, :], rbias).then_inc(s_const, 16)
            sp.dma_start(gate_in[:, :], gates).then_inc(s_const, 16)
            for i in range(PARTS):
                if i >= 2:
                    sp.wait_ge(s_shared, i - 1)
                sp.dma_start(raw[:, i % 2 * PART:(i % 2 + 1) * PART], wall[:, i * PART:(i + 1) * PART]).then_inc(s_sraw[i % 2], 16)

            def attention_io(b, more):
                if more:
                    sp.wait_ge(s_ctx_l, b + 1)
                    load_ctx(b + 1)
                for t in range(TB):
                    sp.wait_ge(s_xn, b * TB + (t + 1))
                    sp.dma_start(xn_t[bass.ds(b * TB + t, 1)].rearrange("o p d -> p o d"),
                                 rows[:, t % 2:t % 2 + 1, :]).then_inc(s_xn_st[t % 2], 16)

            sp.wait_ge(s_x, 16)
            load_x(1)
            attention_io(0, True)
            for b in range(2, B):
                sp.wait_ge(s_x, 16 * b)
                load_x(b)
            sp.wait_ge(s_zero, 2)
            sp.dma_start(xs_dram.rearrange("(t p) d -> p t d", p=P),
                         blank[:, :].rearrange("p (o d) -> p o d", o=1).broadcast_to([P, RT, XW])).then_inc(s_fill, 16)
            attention_io(1, True)
            with sp.Fori(2, B - 1) as b:
                attention_io(b, True)
                store_x2(b - 2, b * TB + (1 - TB))
            attention_io(B - 1, False)
            store_x2(B - 3, TT - 2 * TB + 1)

            def load_xs(t, k):
                sp.dma_start(xs[:, k:k + 1, :], xs_t[bass.ds(t, 1), :, 0:D].rearrange("o p d -> p o d")).then_inc(s_xs[k], 16)

            def load_tag(t, k):
                sp.dma_start(tag[:, k:k + 1, :], xs_t[bass.ds(t, 1), :, D:XW].rearrange("o p d -> p o d")).then_inc(s_tag_in[k], 16)

            sp.wait_ge(s_xm_ps, TT)
            for k in range(2):
                sp.wait_ge(s_xn_st[k], 16 + 16 * TT // 2)
            def load_raw(e, n):
                lo, w = PIECES[n]
                sp.dma_start(raw[:, n * W2C:n * W2C + w], wall[:, bass.ds(e * WC + (2 * WC + lo), w)]).then_inc(s_wraw[n], 16)

            def load_xd(t):
                sp.dma_start(xd[:, t % 4, 0:D], xn_t[t]).then_inc(s_xd[t % 4], 16)

            for n in range(3):
                load_raw(0, n)
            for t in range(4):
                load_xd(t)
            for n in range(3):
                sp.wait_ge(s_wlo, n + 1)
                load_raw(1, n)
            sp.wait_ge(s_tags, 1)
            for t in range(TT):
                if t >= 4:
                    sp.wait_ge(s_sc[t % 4], 32 * (t // 4))
                    load_xd(t)
                sp.dma_start(xd[:, t % 4, D:XW], tags[:, t, :]).then_inc(s_xd[t % 4], 16)
            for k in range(4):
                sp.wait_ge(s_sc[k], 2 * 16 * TT // 4)
            for t in range(2):
                load_xs(t, t)
                load_tag(t, t)
            store_x2(B - 2, TT - TB + 1)
            for t in range(2, 4):
                sp.wait_ge(s_xT_ps, t - 1)
                load_xs(t, t % 2)
            store_x2(B - 1, YACC)
            for n in range(3):
                sp.wait_ge(s_wlo, 3 + n + 1)
                load_raw(2, n)

            def ahead(t, k):
                sp.wait_ge(s_xT_ps, t + 3)
                load_xs(t + 4, k % 2)
                sp.wait_ge(s_added, t * 16 + 16)
                load_tag(t + 2, (k + 2) % 4)

            def raw_following(t):
                e = sp.value_load(load_tab[0:1, FOLLOWING, bass.ds(t, 1)], min_val=0, max_val=E - 1)
                with sp.If(e > 0):
                    e = sp.value_load(load_tab[0:1, FOLLOWING, bass.ds(t, 1)], min_val=1, max_val=E - 1)
                    for n in range(3):
                        wait_alone(sp, s_wlo, e * 3)
                        load_raw(e, n)

            sp.wait_ge(s_route, 1)
            for t in range(4):
                ahead(t, t)
                if t == 1:
                    for n in range(3):
                        sp.wait_ge(s_wlo, 6 + n + 1)
                        load_raw(3, n)
                if t >= 2:
                    raw_following(t)
            with sp.Fori(1, LT // 4 - 1) as j:
                for k in range(4):
                    ahead(j * 4 + k, k)
                    raw_following(j * 4 + k)
            n_used = sp.value_load(used[0:1, :], min_val=LT, max_val=RT)
            for t in range(LT - 4, LT - 2):
                ahead(t, t % 4)
                raw_following(t)
            for t in range(LT - 2, RT - 2):
                with sp.If(n_used > t + 2):
                    if t < RT - 4:
                        ahead(t, t % 4)
                    else:
                        sp.wait_ge(s_added, t * 16 + 16)
                        load_tag(t + 2, (t + 2) % 4)
                raw_following(t)
            wait_alone(sp, s_added, n_used * 16 + 32)

        @block.gpsimd
        def _(pool):
            gp = nc.gpsimd

            gp.memset(ident[:, :], 0.0).then_inc(s_pool_c, 1)
            gp.memset(blank[:, :], 0.0).then_inc(s_zero, 1)
            pool.wait_ge(s_pool_c, 1)
            gp.affine_select(out=ident[:, :], in_=ident[:, :], compare_op=ALU.not_equal, fill=1.0,
                             base=0, pattern=[[-1, P]], channel_multiplier=1).then_inc(s_pool_c, 1)
            gp.memset(neg_half[:, :], -0.5).then_inc(s_pool_c, 1)
            imprecise = dict(channel_multiplier=0, allow_small_or_imprecise_dtypes=True)
            gp.iota(iota_e[:, :], pattern=[[1, E]], base=0, **imprecise)
            gp.iota(iota_t[:, :], pattern=[[1, RT + 1]], base=0, **imprecise)
            gp.iota(iota_k[:, :], pattern=[[P, TT]], base=0, **imprecise)
            gp.iota(tags[:, :, 0].bitcast(I32), pattern=[[P, TT]], base=0, channel_multiplier=1)
            gp.memset(below[:, :, :], 1.0).then_inc(s_pool_c, 1)
            gp.memset(step_r[:, :], 1.0).then_inc(s_pool_c, 1)
            gp.memset(upper_f[:, :], 1.0).then_inc(s_pool_c, 1)
            pool.wait_ge(s_zero, 1)
            gp.iota(blank[:, D:D + 1].bitcast(I32), pattern=[[0, 1]], base=TT * P, channel_multiplier=1).then_inc(s_zero, 1)
            for k in range(2):
                lo, hi = k * P // 2, (k + 1) * P // 2
                pool.dma_start(out[TT * P + lo:TT * P + hi], blank[lo:hi, 0:D]).then_inc(s_added, 16)
            pool.wait_ge(s_pool_c, 6)
            for e in range(1, E):
                if (e + 2) % RING == 0:
                    gp.memset(step_r[:, e - 1:e], 1.0 - RING)
            gp.affine_select(out=below[:, :, :], in_=below[:, :, :], compare_op=ALU.is_gt, fill=0.0,
                             base=0, pattern=[[1, E], [-1, E]], channel_multiplier=0)
            gp.affine_select(out=upper_f[:, :], in_=upper_f[:, :], compare_op=ALU.is_gt, fill=0.0,
                             base=0, pattern=[[1, P]], channel_multiplier=-1).then_inc(s_pool_c, 1)

            def context_lo(b):
                pool.wait_ge(s_ctx_h, b + 1)
                gp.tensor_tensor(ctx_l[:, :, :].rearrange("p c l -> p (c l)"), ctx_f[:, :],
                                 f(ctx_h[:, :, :].rearrange("p c l -> p (c l)")), ALU.subtract).then_inc(s_ctx_l, 1)

            def rstd_1(b):
                wait_alone(pool, s_bn1, b + 1)
                gp.tensor_scalar(ve[:, :], mv[:, :, 1], EPS, None, ALU.add).then_inc(s_pool_1, 1)
                gp.tensor_scalar(mv[:, :, 0], mv[:, :, 0], -1.0, None, ALU.mult).then_inc(s_pool_1, 1)
                pool.wait_ge(s_pool_1, b * 3 + 2)
                gp.tensor_tensor(rstd[:, :], ve[:, :], neg_half[:, :], ALU.pow).then_inc(s_pool_1, 1)
                pool.wait_ge(s_pool_1, b * 3 + 3)
                gp.tensor_tensor(nb[:, :], mv[:, :, 0], rstd[:, :], ALU.mult).then_inc(s_rstd1, 1)

            def rstd_2(b, t):
                two = slice(t, t + 2)
                wait_alone(pool, s_bn2, b * TB + (t + 2))
                gp.tensor_scalar(ve2[:, two], mv2[:, two, 1], EPS, None, ALU.add).then_inc(s_pool, 1)
                gp.tensor_scalar(mv2[:, two, 0], mv2[:, two, 0], -1.0, None, ALU.mult).then_inc(s_pool, 1)
                pool.wait_ge(s_pool, b * 6 + (2 + 3 * (t // 2)))
                gp.tensor_tensor(rstd2[:, two], ve2[:, two], neg_half[:, two], ALU.pow).then_inc(s_pool, 1)
                pool.wait_ge(s_pool, b * 6 + (3 + 3 * (t // 2)))
                gp.tensor_tensor(nb2[:, two], mv2[:, two, 0], rstd2[:, two], ALU.mult).then_inc(s_rstd2, 1)

            def load_part(i):
                part = slice(i * PART, (i + 1) * PART)
                pool.dma_start(ring_h[:, part], wall[:, part]).then_inc(s_shi[i % 4], 16)

            def split_part(i):
                part = slice(i * PART, (i + 1) * PART)
                pool.wait_ge(s_sraw[i % 2], 16 * (i // 2 + 1))
                pool.wait_ge(s_shi[i % 4], 16 * (i // 4 + 1))
                gp.tensor_tensor(ring_l[:, part], raw[:, i % 2 * PART:(i % 2 + 1) * PART], f(ring_h[:, part]),
                                 ALU.subtract).then_inc(s_shared, 1)
                if i + 4 < PARTS:
                    load_part(i + 4)

            context_lo(0)
            rstd_1(0)
            for i in range(4):
                load_part(i)
            for i in range(PARTS):
                split_part(i)
            context_lo(1)
            rstd_1(1)
            rstd_2(0, 0)
            rstd_2(0, 2)
            with pool.Fori(1, B) as b:
                with pool.If(b < B - 1):
                    context_lo(b + 1)
                    rstd_1(b + 1)
                rstd_2(b, 0)
                rstd_2(b, 2)

            def split_weights(e, at):
                load_hi(e, at, range(3))
                for n in range(3):
                    split_piece(e, at, n)

            def load_hi(e, at, pieces):
                for n in pieces:
                    lo, w = PIECES[n]
                    pool.dma_start(ring_h[:, bass.ds(at + lo, w)], wall[:, bass.ds(e * WC + (2 * WC + lo), w)]).then_inc(s_whi[n], 16)

            def split_piece(e, at, n):
                lo, w = PIECES[n]
                wait_alone(pool, s_wraw[n], e * 16 + 16)
                wait_alone(pool, s_whi[n], e * 16 + 16)
                part = bass.ds(at + lo, w)
                gp.tensor_tensor(ring_l[:, part], raw[:, n * W2C:n * W2C + w], f(ring_h[:, part]),
                                 ALU.subtract).then_inc(s_wlo, 1)

            split_weights(0, 2 * WC)

            pool.wait_ge(s_fill, 16)
            pool.wait_ge(s_slot, 1)
            for t in range(TT):
                pool.wait_ge(s_xd[t % 4], 32 * (t // 4 + 1))
                for k in range(2):
                    pool.indirect_dma_start(xs_dram, bass.IndirectOffsetOnAxis(slot[:, k, t:t + 1], 0),
                                            xd[:, t % 4, :], None).then_inc(s_sc[t % 4], 16)

            pool.wait_ge(s_y, TT)
            split_weights(1, 0)
            pool.wait_ge(s_y, Y0)
            split_weights(2, WC)

            pool.wait_ge(s_route, 1)
            pool.wait_ge(s_out, 16 * B)

            def add_tile(t, k):
                wait_alone(pool, s_ycp, t + 3)
                wait_alone(pool, s_added, t * 16 + 32)
                pool.indirect_dma_start(out, bass.IndirectOffsetOnAxis(tag[:, k, 0:1].bitcast(U32), 0),
                                        ysb[:, k % 2, :], None, compute_op=ALU.add).then_inc(s_added, 16)

            def next_hi(t):
                e = pool.value_load(load_tab[0:1, LOAD, bass.ds(t + 2, 1)], min_val=0, max_val=E - 1)
                with pool.If(e > 0):
                    at = pool.value_load(load_tab[0:1, INTO, bass.ds(t + 2, 1)], min_val=0, max_val=(RING - 1) * WC)
                    load_hi(e, at, (0, 1))

            def next_lo(t, back, pieces):
                place = bass.ds(t + (2 - back), 1)
                e = pool.value_load(load_tab[0:1, LOAD, place], min_val=0, max_val=E - 1)
                with pool.If(e > 0):
                    e = pool.value_load(load_tab[0:1, LOAD, place], min_val=RING, max_val=E - 1)
                    at = pool.value_load(load_tab[0:1, INTO, place], min_val=0, max_val=(RING - 1) * WC)
                    if 2 not in pieces:
                        load_hi(e, at, (2,))
                    for n in pieces:
                        split_piece(e, at, n)

            def step(t, k):
                next_lo(t, 2, (2,))
                next_lo(t, 1, (0, 1))
                add_tile(t, k)
                next_hi(t)

            with pool.Fori(0, LT // 4) as j:
                for k in range(4):
                    step(j * 4 + k, k)
            n_used = pool.value_load(used[0:1, :], min_val=LT, max_val=RT)
            for t in range(LT, RT):
                if t < RT - 1:
                    next_lo(t, 2, (2,))
                if t < RT - 2:
                    next_lo(t, 1, (0, 1))
                with pool.If(n_used > t):
                    add_tile(t, t % 4)
                if t < RT - 3:
                    next_hi(t)

        @block.scalar
        def _(act):
            a = nc.scalar
            act.wait_ge(s_wqk, 16)
            a.activation(wqk_h[:, :, :].rearrange("p c n -> p (c n)"), wqk_f, ACT.Copy).then_inc(s_wqk_h, 1)

            def context_hi(b):
                act.wait_ge(s_ctx, b * 16 + 16)
                a.activation(ctx_h[:, :, :].rearrange("p c l -> p (c l)"), ctx_f[:, :], ACT.Copy).then_inc(s_ctx_h, 1)

            context_hi(0)
            act.wait_ge(s_const, 16 * 3)
            a.activation(tg[:, :], gate_in[:, :], ACT.Tanh).then_inc(s_tanh, 1)

            def copy_hi(dst, src, ready, count, done):
                act.wait_ge(ready, count)
                a.activation(dst, src, ACT.Copy).then_inc(done, 1)

            def hidden(u):
                act.wait_ge(s_h1, u + 1)
                act.wait_ge(s_g, u + 1)
                a.activation(silu[:, :], b_h1[:, 0:F], ACT.Tanh, scale=0.5).then_inc(s_th, 1)

            def gT_hi(u):
                act.wait_ge(s_gT_ps, u + 1)
                a.activation(gT_h[:, :, :].rearrange("p c n -> p (c n)")[:, 0:2 * P], b_gT[:, 0:2 * P], ACT.Copy)
                a.activation(gT_h[0:FCH[2], 2, :], b_gT[0:FCH[2], 2 * P:3 * P], ACT.Copy).then_inc(s_gT_h, 1)

            def attention(b, shared):
                def tile(t):
                    return acc[:, bass.ds(b * TB * D + t * D, D)]

                def stage_N(t):
                    if t == 0:
                        wait_alone(act, s_rstd1, b + 1)
                    if t < 2:
                        wait_alone(act, s_xn_st[t], b * 32 + 16)
                    a.activation(rows[:, t % 2, :], tile(t), ACT.Identity, bias=nb[:, t:t + 1],
                                 scale=rstd[:, t:t + 1]).then_inc(s_lnx, 1)

                def stage_Q(k):
                    act.wait_ge(s_q_ps, b * 2 + (k + 1))
                    a.activation(qk_h[:, k, :], b_of[f"Q{k}"][:, :], ACT.Identity, bias=bias_qk[:, k:k + 1]).then_inc(s_q_h, 1)

                def stage_L(t):
                    copy_hi(lnxT_h[:, :, t * P:(t + 1) * P], b_of[f"L{t}"][:, :].rearrange("p (c l) -> p c l", c=TB),
                            s_lx_ps, b * TB + (t + 1), s_lx_h)

                def stage_E(t):
                    act.wait_ge(s_max, b * TB + (t + 1))
                    a.activation(att[:, t % 2, :], b_of[f"E{t}"][:, :], ACT.Exp, bias=nmax[:, t:t + 1],
                                 accum_out=esum[:, t:t + 1]).then_inc(s_exp, 1)

                def stage_D(t):
                    act.wait_ge(s_rsum, b * TB + (t + 1))
                    a.activation(att[:, t % 2, :], att[:, t % 2, :], ACT.Copy, scale=rsum[:, t:t + 1]).then_inc(s_att, 1)

                def stage_A(t):
                    copy_hi(attT_h[:, :, t * P:(t + 1) * P], b_of[f"A{t}"][:, :].rearrange("p (c l) -> p c l", c=TB),
                            s_at_ps, b * TB + (t + 1), s_at_h)

                def stage_R(t):
                    if t % 2 == 0:
                        wait_alone(act, s_rstd2, b * 2 + (t // 2 + 1))
                    if t >= 2:
                        wait_alone(act, s_xn_st[t % 2], b * 32 + 32)
                    a.activation(rows[:, t % 2, :], tile(t), ACT.Identity, bias=nb2[:, t:t + 1],
                                 scale=rstd2[:, t:t + 1]).then_inc(s_xn, 1)

                def stage_T(t):
                    copy_hi(xTs_h[:, t, :], b_of[f"T{t}"][:, :], s_xt_ps, b * TB + (t + 1), s_xt_h)

                def stage_C(_):
                    if not shared:
                        context_hi(1)
                    else:
                        with act.If(b < B - 1):
                            context_hi(b + 1)

                stages = {"N": stage_N, "Q": stage_Q, "L": stage_L, "E": stage_E, "D": stage_D, "A": stage_A,
                          "R": stage_R, "T": stage_T, "C": stage_C}
                if shared:
                    stages |= {"U": lambda q: hidden(b * 8 + (q - 8)), "V": lambda q: gT_hi(b * 8 + (q - 8))}
                for name in ORDER:
                    if name[0] in stages:
                        stages[name[0]](int(name[1]))

            act.sem_inc(s_g, 1)
            act.sem_inc(s_ycp, 2)
            attention(0, False)
            with act.Fori(1, B) as b:
                attention(b, True)

            u0 = 8 * (B - 1)
            act.wait_ge(s_xn_st[0], 16 + 16 * TT // 2)
            act.wait_ge(s_xn_st[1], 16 + 16 * TT // 2)
            act.wait_ge(s_fill, 16)
            act.wait_ge(s_g, u0 + 1)
            a.activation(score[:, 0:TT - TB, :].rearrange("p t e -> p (t e)"), logits[:, 0:(TT - TB) * E], ACT.Sigmoid).then_inc(s_score, 1)
            act.wait_ge(s_lg, 1)
            a.activation(score[:, TT - TB:TT, :].rearrange("p t e -> p (t e)"), logits[:, (TT - TB) * E:TT * E], ACT.Sigmoid).then_inc(s_score, 1)

            hidden(u0)
            for q in range(1, 8):
                hidden(u0 + q)
                gT_hi(u0 + q - 1)

            def hidden_silu(u):
                act.wait_ge(s_h1, u + 1)
                act.wait_ge(s_g, u + 1)
                a.activation(silu[:, :], b_h1[:, 0:F], ACT.Silu).then_inc(s_silu, 1)

            def xT_hi(n):
                act.wait_ge(s_xT_ps, n + 1)
                a.activation(xT_h[:, :, :].rearrange("p c n -> p (c n)"), b_xT[:, :], ACT.Copy).then_inc(s_xT_h, 1)

            xT_hi(0)
            hidden_silu(2 * TT)
            gT_hi(2 * TT - 1)
            xT_hi(1)

            def routed(t, k, j, nxt, turn):
                if nxt:
                    hidden_silu(t + (2 * TT + 1))
                gT_hi(t + 2 * TT)
                if turn:
                    xT_hi(t + 2)
                column = act.value_load(tile_tab[0:1, COLUMN, bass.ds(t, 1)], min_val=1, max_val=E)
                wait_alone(act, s_y, t + (Y0 + 1))
                wait_alone(act, s_tag_in[k], j * 16 + 16)
                wait_alone(act, s_added, t * 16 + 16)
                a.activation(ysb[:, k % 2, :], b_y[k % 2][:, :], ACT.Copy,
                             scale=tag[:, k, bass.ds(column, 1)]).then_inc(s_ycp, 1)

            act.wait_ge(s_route, 1)
            with act.Fori(0, LT // 4) as j:
                for k in range(4):
                    routed(j * 4 + k, k, j, True, True)
            n_used = act.value_load(used[0:1, :], min_val=LT, max_val=RT)
            for t in range(LT, RT):
                with act.If(n_used > t):
                    routed(t, t % 4, t // 4, t + 1 < RT, t + 2 < RT)

        @block.vector
        def _(dve):
            v = nc.vector
            chain = {"n": 0}

            def link(ins, base=0):
                chain["n"] += 1
                ins.then_inc(s_dve, 1)
                if isinstance(base, int):
                    dve.wait_ge(s_dve, base + chain["n"])
                else:
                    wait_alone(dve, s_dve, base + chain["n"])

            dve.wait_ge(s_wqk_h, 1)
            v.tensor_tensor(wqk_l[:, :, :].rearrange("p c n -> p (c n)"), wqk_f,
                            f(wqk_h[:, :, :].rearrange("p c n -> p (c n)")), ALU.subtract).then_inc(s_wqk_l, 1)
            per_b = TB

            def half(u, b=None, q=None):
                dve.wait_ge(s_th, u + 1)
                if b is not None:
                    copy_logits(b, q)
                v.scalar_tensor_tensor(out=silu[:, :], in0=silu[:, :], scalar=1.0, in1=b_h1[:, 0:F],
                                       op0=ALU.add, op1=ALU.mult).then_inc(s_silu, 1)

            def shared_product(u):
                dve.wait_ge(s_silu, u + 2)
                dve.wait_ge(s_h3, u + 1)
                v.scalar_tensor_tensor(out=g[:, :], in0=silu[:, :], scalar=0.5, in1=b_h3[:, 0:F],
                                       op0=ALU.mult, op1=ALU.mult).then_inc(s_g, 1)

            def gT_lo(u):
                dve.wait_ge(s_gT_h, u + 1)
                v.tensor_tensor(gT_l[:, :, :].rearrange("p c n -> p (c n)")[:, 0:2 * P], b_gT[:, 0:2 * P],
                                f(gT_h[:, :, :].rearrange("p c n -> p (c n)")[:, 0:2 * P]), ALU.subtract)
                v.tensor_tensor(gT_l[0:FCH[2], 2, :], b_gT[0:FCH[2], 2 * P:3 * P], f(gT_h[0:FCH[2], 2, :]),
                                ALU.subtract).then_inc(s_gT_l, 1)

            def add_shared(n, count, k=0):
                tile = acc[:, bass.ds(n * D, D)]
                dve.wait_ge(s_y, count + 1)
                v.scalar_tensor_tensor(out=tile, in0=b_y[k][:, :], scalar=tg[:, 1:2], in1=tile,
                                       op0=ALU.mult, op1=ALU.add).then_inc(s_yacc, 1)

            def copy_logits(b, q):
                if q % 2 == 0:
                    v.tensor_copy(logits[:, bass.ds(b * TB * E + (q // 2 - TB) * E, E)], b_h1[:, F:F + E])

            def sub_hi(dst, src, hi, ready, count, done):
                dve.wait_ge(ready, count)
                v.tensor_tensor(dst, src, f(hi), ALU.subtract).then_inc(done, 1)

            def mean_variance(b):
                wait_alone(dve, s_x, b * 16 + 16)
                for t in range(TB):
                    o = v.bn_stats(st[:, t, :], acc[:, bass.ds(b * TB * D + t * D, D)])
                o.then_inc(s_st, 1)
                wait_alone(dve, s_st, b + 1)
                for t in range(TB):
                    o = v.bn_aggr(mv[:, t, :], st[:, t, :])
                o.then_inc(s_bn1, 1)

            def attention(b, shared):
                chain["n"] = 0
                base = b * per_b

                def tile(t):
                    return acc[:, bass.ds(b * TB * D + t * D, D)]

                def cols(t):
                    return slice(t * P, (t + 1) * P)

                def stage_Q(k):
                    dve.wait_ge(s_q_h, b * 2 + (k + 1))
                    v.scalar_tensor_tensor(out=qk_l[:, k, :], in0=b_of[f"Q{k}"][:, :], scalar=bias_qk[:, k:k + 1],
                                           in1=f(qk_h[:, k, :]), op0=ALU.add, op1=ALU.subtract).then_inc(s_q_l, 1)

                def stage_L(t):
                    sub_hi(lnxT_l[:, :, cols(t)], b_of[f"L{t}"][:, :].rearrange("p (c l) -> p c l", c=TB),
                           lnxT_h[:, :, cols(t)], s_lx_h, b * TB + (t + 1), s_lx_l)

                def stage_E(t):
                    dve.wait_ge(s_e_ps, b * TB + (t + 1))
                    v.tensor_reduce(nmax[:, t:t + 1], b_of[f"E{t}"][:, :], AX, ALU.max, negate=True).then_inc(s_max, 1)

                def stage_D(t):
                    dve.wait_ge(s_exp, b * TB + (t + 1))
                    v.reciprocal(rsum[:, t:t + 1], esum[:, t:t + 1]).then_inc(s_rsum, 1)

                def stage_A(t):
                    sub_hi(attT_l[:, :, cols(t)], b_of[f"A{t}"][:, :].rearrange("p (c l) -> p c l", c=TB),
                           attT_h[:, :, cols(t)], s_at_h, b * TB + (t + 1), s_at_l)

                def stage_M(t):
                    if t == 0 and not shared:
                        dve.wait_ge(s_tanh, 1)
                    dve.wait_ge(s_xm_ps, b * TB + (t + 1))
                    v.scalar_tensor_tensor(out=tile(t), in0=b_of[f"M{t}"][:, :], scalar=tg[:, 0:1], in1=tile(t),
                                           op0=ALU.mult, op1=ALU.add).then_inc(s_x1, 1)
                    wait_alone(dve, s_x1, b * TB + (t + 1))
                    link(v.bn_stats(st[:, TB + t, :], tile(t)), base)
                    v.bn_aggr(mv2[:, t, :], st[:, TB + t, :]).then_inc(s_bn2, 1)

                def stage_T(t):
                    sub_hi(xTs_l[:, t, :], b_of[f"T{t}"][:, :], xTs_h[:, t, :], s_xt_h, b * TB + (t + 1), s_xt_l)

                def stage_C(_):
                    if not shared:
                        mean_variance(1)
                    else:
                        with dve.If(b < B - 1):
                            mean_variance(nc.s_assert_within(b + 1, 2, B - 1, skip_runtime_bounds_check_because="only where b < B - 1"))

                stages = {"Q": stage_Q, "L": stage_L, "E": stage_E, "D": stage_D, "A": stage_A, "M": stage_M, "T": stage_T,
                          "C": stage_C}
                if shared:
                    stages |= {"U": lambda q: half(b * 8 + (q - 8), b, q), "X": lambda q: shared_product(b * 8 + (q - 8)),
                               "V": lambda q: gT_lo(b * 8 + (q - 8)),
                               "W": lambda q: add_shared(b * TB + (q // 2 - TB), b * TB + (q // 2 - TB)) if q % 2 else None}
                for name in ORDER:
                    if name[0] in stages:
                        stages[name[0]](int(name[1]))

            dve.sem_inc(s_silu, 1)
            dve.sem_inc(s_yacc, 1)
            mean_variance(0)
            attention(0, False)
            with dve.Fori(1, B) as b:
                attention(b, True)

            u0 = 8 * (B - 1)
            base = B * per_b
            chain["n"] = 0

            def over(ap, n):
                return ap.rearrange("p (o k) -> p o k", o=1).broadcast_to([P, n, ap.shape[1]])

            def top_two(start, stop):
                link(v.tensor_tensor(sel[:, start:stop, :], score[:, start:stop, :], over(rb[:, :], stop - start), ALU.add), base)
                for t in range(start, stop):
                    o = v.max(top8[:, t, :], sel[:, t, :])
                link(o, base)
                for t in range(start, stop):
                    o = v.max_index(idx8[:, t, :], top8[:, t, :], sel[:, t, :])
                return o

            dve.wait_ge(s_pool_c, 7)
            dve.wait_ge(s_score, 1)
            top_two(0, TT - TB)
            dve.wait_ge(s_lg_ps, 1)
            v.tensor_copy(logits[:, (TT - TB) * E:TT * E], b_of["G"][:, 0:TB * E]).then_inc(s_lg, 1)
            dve.wait_ge(s_score, 2)
            link(top_two(TT - TB, TT), base)
            link(v.tensor_copy(idxf[:, :, :], idx8[:, :, 0:2]), base)
            ie = over(iota_e[:, :], TT)
            for k in range(2):
                o = v.tensor_tensor(one_hot[k][:, :, :], ie, idxf[:, :, k:k + 1].broadcast_to([P, TT, E]), ALU.is_equal)
            link(o, base)
            v.tensor_copy(upper[:, :], upper_f[:, :])
            v.memset(f(ones[:, :]), 1.0)
            v.tensor_tensor(mask[:, :].rearrange("p (t e) -> p t e", t=TT), one_hot[0][:, :, :], one_hot[1][:, :, :], ALU.add).then_inc(s_mask, 1)
            half(u0)
            weighted = tags[:, :, 1:TAG]
            link(v.tensor_tensor(tmp[:, :, :], one_hot[0][:, :, :], one_hot[1][:, :, :], ALU.add), base)
            link(v.tensor_tensor(weighted, tmp[:, :, :], score[:, :, :], ALU.mult), base)
            link(v.tensor_reduce(wsum[:, :], weighted, AX, ALU.add), base)
            link(v.tensor_scalar(wsum[:, :], wsum[:, :], 1e-12, None, ALU.max), base)
            link(v.reciprocal(wsum[:, :], wsum[:, :]), base)
            link(v.tensor_tensor(weighted, weighted, wsum[:, :].rearrange("p (t o) -> p t o", o=1).broadcast_to([P, TT, E]), ALU.mult), base)
            v.tensor_scalar(weighted, weighted, tg[:, 1:2], None, ALU.mult).then_inc(s_tags, 1)
            shared_product(u0)

            def add_last(i):
                if i >= TB:
                    dve.wait_ge(s_yacc, TT - 2 * TB + i + 2)
                add_shared(TT - TB + i % TB, TT - TB + i, i % 2)

            def shared_step(q):
                half(u0 + q)
                gT_lo(u0 + q - 1)
                shared_product(u0 + q)
                if q >= 2:
                    add_last(q - 2)

            dve.wait_ge(s_rank_ps, 1)
            v.tensor_copy(cnt[:, :, :].rearrange("p t e -> p (t e)"), b_rank[1][:, 0:TT * E])
            link(v.tensor_copy(pre[0][:, :, :].rearrange("p t e -> p (t e)"), b_rank[1][:, 0:TT * E]), base)
            s, k = 1, 0
            while s < TT:
                v.tensor_copy(pre[1 - k][:, 0:s, :], pre[k][:, 0:s, :])
                link(v.tensor_tensor(pre[1 - k][:, s:, :], pre[k][:, s:, :], pre[k][:, 0:TT - s, :], ALU.add), base)
                s, k = 2 * s, 1 - k
            incl = pre[k]
            total = incl[:, TT - 1:TT, :].rearrange("p o e -> p e o")
            cmp = tmp[:, :, :].rearrange("p t e -> p (t e)").rearrange("p (e t) -> p e t", e=E)
            link(v.tensor_tensor(cmp, total.broadcast_to([P, E, TT]), over(iota_k[:, :], E), ALU.is_gt), base)
            link(v.tensor_reduce(ntile[:, :], cmp, AX, ALU.add), base)
            link(v.tensor_scalar(ntile[:, :], ntile[:, :], 1.0, None, ALU.max), base)
            less = tmp[:, 0:E, :]
            link(v.tensor_tensor(less, below[:, :, :], over(ntile[:, :], E), ALU.mult), base)
            link(v.tensor_reduce(first[:, :], less, AX, ALU.add), base)
            link(v.tensor_scalar(first_r[:, :], first[:, :], float(P), None, ALU.mult), base)
            link(v.tensor_tensor(cnt[:, :, :], incl[:, :, :], cnt[:, :, :], ALU.subtract), base)
            link(v.tensor_tensor(cnt[:, :, :], cnt[:, :, :], over(first_r[:, :], TT), ALU.add), base)
            link(v.tensor_tensor(cnt[:, :, :].rearrange("p t e -> p (t e)"), b_rank[0][:, 0:TT * E],
                                 cnt[:, :, :].rearrange("p t e -> p (t e)"), ALU.add), base)
            for k in range(2):
                link(v.tensor_tensor(tmp[:, :, :], one_hot[k][:, :, :], cnt[:, :, :], ALU.mult), base)
                link(v.tensor_reduce(slot_f[:, :], tmp[:, :, :], AX, ALU.add), base)
                link(v.tensor_copy(slot[:, k, :], slot_f[:, :]), base)
            dve.sem_inc(s_slot, 1)
            shared_step(1)
            shared_step(2)
            fe = over(first[:, 1:E], RT + 1)
            link(v.tensor_tensor(passed[:, :, :], iota_t[:, :].rearrange("p (t o) -> p t o", o=1).broadcast_to([P, RT + 1, E - 1]), fe, ALU.is_ge), base)
            link(v.tensor_reduce(tile_f[:, 1, :], passed[:, :, :], AX, ALU.add), base)
            link(v.tensor_tensor(passed[:, :, :], passed[:, :, :],
                                 over(step_r[:, 0:E - 1], RT + 1), ALU.mult), base)
            link(v.tensor_reduce(tile_f[:, 0, :], passed[:, :, :], AX, ALU.add), base)
            expert = tile_f[:, 1, :]
            link(v.tensor_scalar(tile_f[:, 0, :], tile_f[:, 0, :], float(WC), 2.0 * WC, ALU.mult, ALU.add), base)
            v.tensor_copy(tile_tab[:, IN_RING, :], tile_f[:, 0, :])
            v.tensor_scalar(tile_tab[:, SPLIT, :], expert, 3.0, 3.0, ALU.mult, ALU.add)
            v.tensor_scalar(tile_tab[:, COLUMN, :], expert, 1.0, None, ALU.add)
            v.memset(tile_f[:, 2:4, RT:RT + 1], 0.0)
            v.tensor_tensor(tile_f[:, 2, 0:RT], tile_f[:, 1, 1:RT + 1], tile_f[:, 1, 0:RT], ALU.subtract)
            link(v.tensor_scalar(tile_f[:, 3, 0:RT], tile_f[:, 1, 0:RT], float(RING), None, ALU.add), base)
            link(v.tensor_tensor(tile_f[:, 2, :], tile_f[:, 2, :], tile_f[:, 3, :], ALU.mult), base)
            link(v.tensor_scalar(tile_f[:, 3, :], tile_f[:, 2, :], float(E), None, ALU.is_lt), base)
            link(v.tensor_tensor(tile_f[:, 2, :], tile_f[:, 2, :], tile_f[:, 3, :], ALU.mult), base)
            v.memset(load_tab[:, :, 0:2], 0)
            link(v.tensor_reduce(wsum[:, 0:1], ntile[:, :], AX, ALU.add), base)
            v.tensor_copy(used[:, :], wsum[:, 0:1])
            v.tensor_copy(load_tab[:, LOAD, 2:RT + 2], tile_f[:, 2, 0:RT])
            v.tensor_copy(load_tab[:, INTO, 2:RT + 2], tile_f[:, 0, 0:RT])
            link(v.tensor_scalar(tile_f[:, 1, :], tile_f[:, 2, :], 1.0, None, ALU.add), base)
            link(v.tensor_scalar(tile_f[:, 0, :], tile_f[:, 2, :], 0.0, None, ALU.is_gt), base)
            link(v.tensor_tensor(tile_f[:, 1, :], tile_f[:, 1, :], tile_f[:, 0, :], ALU.mult), base)
            link(v.tensor_scalar(tile_f[:, 0, :], tile_f[:, 1, :], float(E), None, ALU.is_lt), base)
            link(v.tensor_tensor(load_tab[:, FOLLOWING, 2:RT + 2], tile_f[:, 1, 0:RT], tile_f[:, 0, 0:RT], ALU.mult), base)
            dve.sem_inc(s_route, 1)

            for q in range(3, 8):
                shared_step(q)

            def xT_lo(n):
                dve.wait_ge(s_xT_h, n + 1)
                v.tensor_tensor(xT_l[:, :, :].rearrange("p c n -> p (c n)"), b_xT[:, :],
                                f(xT_h[:, :, :].rearrange("p c n -> p (c n)")), ALU.subtract).then_inc(s_xT_l, 1)

            def product(u):
                dve.wait_ge(s_silu, u + 2)
                dve.wait_ge(s_h3, u + 1)
                v.tensor_tensor(g[:, :], silu[:, :], b_h3[:, 0:F], ALU.mult).then_inc(s_g, 1)

            xT_lo(0)
            gT_lo(2 * TT - 1)
            product(2 * TT)
            xT_lo(1)
            add_last(2 * TB - 2)
            add_last(2 * TB - 1)

            def routed(t, nxt, turn):
                gT_lo(t + 2 * TT)
                if nxt:
                    product(t + (2 * TT + 1))
                if turn:
                    xT_lo(t + 2)

            with dve.Fori(0, LT // 2) as j:
                for k in range(2):
                    routed(j * 2 + k, True, True)
            n_used = dve.value_load(used[0:1, :], min_val=LT, max_val=RT)
            for t in range(LT, RT):
                with dve.If(n_used > t):
                    routed(t, t + 1 < RT, t + 2 < RT)

        @block.tensor
        def _(pe):
            t_ = nc.tensor

            def product3(out, pairs):
                n = 0
                for sh, sl, mh, ml in pairs:
                    for s, m in ((sh, mh), (sh, ml), (sl, mh)):
                        o = t_.matmul(out, s, m, start=(n == 0), stop=(n == 3 * len(pairs) - 1))
                        n += 1
                return o


            def turn(dst, src, s):
                for c in range(4):
                    o = t_.transpose(dst[:, c * P:(c + 1) * P], src[:, c * P:(c + 1) * P], ident[:, :])
                o.then_inc(s, 1)

            def up(which, r, xh, xl, n=F):
                pairs = []
                for c in range(KC):
                    lo = c * UP + which * (F + E)
                    pairs.append((xh[:, c * P:(c + 1) * P], xl[:, c * P:(c + 1) * P],
                                  ring_h[:, bass.ds(r + lo, n)], ring_l[:, bass.ds(r + lo, n)]))
                product3((b_h1, b_h3)[which][:, 0:n], pairs).then_inc((s_h1, s_h3)[which], 1)

            def turn_g(u):
                pe.wait_ge(s_g, u + 2)
                for c, w in enumerate(FCH):
                    o = t_.transpose(b_gT[0:w, c * P:(c + 1) * P], g[:, c * P:c * P + w], ident[:, :])
                o.then_inc(s_gT_ps, 1)

            def down(u, r, k, start, stop):
                pe.wait_ge(s_gT_l, u + 1)
                n, last = 0, 3 * len(FCH) - 1
                for c, w in enumerate(FCH):
                    lo = W13 + c * D
                    mh, ml = ring_h[0:w, bass.ds(r + lo, D)], ring_l[0:w, bass.ds(r + lo, D)]
                    for s, m in ((gT_h[0:w, c, :], mh), (gT_h[0:w, c, :], ml), (gT_l[0:w, c, :], mh)):
                        o = t_.matmul(b_y[k][:, :], s, m, start=(start and n == 0), stop=(stop and n == last))
                        n += 1
                return o

            def shared_up(u, q, which, router=True):
                if which == 0:
                    pe.wait_ge(s_silu, u + 1)
                up(which, q % 2 * WC, xTs_h[:, q // 2, :], xTs_l[:, q // 2, :],
                   F + E if router and q % 2 == 0 and which == 0 else F)

            def shared_down(u, q, n):
                if q % 2 == 0:
                    pe.wait_ge(s_yacc, n + 1)
                o = down(u, q % 2 * WC, 0, q % 2 == 0, q % 2 == 1)
                if q % 2:
                    o.then_inc(s_y, 1)

            def attention(b, shared):
                def stage_Q(k):
                    if k == 0:
                        pe.wait_ge(s_ctx_l, b + 1)
                    cols = slice(k * DQ, (k + 1) * DQ)
                    product3(b_of[f"Q{k}"][:, :], [(wqk_h[:, c, cols], wqk_l[:, c, cols], ctx_h[:, c, :], ctx_l[:, c, :])
                                                   for c in range(CC)]).then_inc(s_q_ps, 1)

                def stage_L(t):
                    pe.wait_ge(s_lnx, b * TB + (t + 1))
                    if t == 2:
                        pe.wait_ge(s_lx_l, b * TB + 2)
                    if t == 3:
                        pe.wait_ge(s_at_l, b * TB + 1)
                    turn(b_of[f"L{t}"], rows[:, t % 2, :], s_lx_ps)

                def stage_E(t):
                    if t == 0:
                        pe.wait_ge(s_q_l, b * 2 + 2)
                    if t == 3:
                        pe.wait_ge(s_lx_l, b * TB + 3)
                    rs = slice(t * P, (t + 1) * P)
                    product3(b_of[f"E{t}"][:, :], [(qk_h[:, 0, rs], qk_l[:, 0, rs], qk_h[:, 1, :], qk_l[:, 1, :])]).then_inc(s_e_ps, 1)

                def stage_A(t):
                    pe.wait_ge(s_att, b * TB + (t + 1))
                    if t == 0:
                        pe.wait_ge(s_lx_l, b * TB + 1)
                    if t == 3:
                        pe.wait_ge(s_at_l, b * TB + 2)
                    turn(b_of[f"A{t}"], att[:, t % 2, :], s_at_ps)

                def stage_M(t):
                    if t == 0:
                        pe.wait_ge(s_lx_l, b * TB + TB)
                        pe.wait_ge(s_at_l, b * TB + TB)
                    rs = slice(t * P, (t + 1) * P)
                    product3(b_of[f"M{t}"][:, :], [(lnxT_h[:, c, rs], lnxT_l[:, c, rs], attT_h[:, c, :], attT_l[:, c, :])
                                                   for c in range(TB)]).then_inc(s_xm_ps, 1)

                def stage_T(t):
                    pe.wait_ge(s_xn, b * TB + (t + 1))
                    turn(b_of[f"T{t}"], rows[:, t % 2, :], s_xt_ps)

                stages = {"Q": stage_Q, "L": stage_L, "E": stage_E, "A": stage_A, "M": stage_M, "T": stage_T}
                if shared:
                    stages |= {"U": lambda q: shared_up(b * 8 + (q - 8), q, 0), "X": lambda q: shared_up(b * 8 + (q - 8), q, 1),
                               "V": lambda q: turn_g(b * 8 + (q - 8)),
                               "W": lambda q: shared_down(b * 8 + (q - 8), q, b * TB + (q // 2 - TB))}
                if shared:
                    pe.wait_ge(s_xt_l, b * TB)
                for name in ORDER:
                    if name[0] in stages:
                        stages[name[0]](int(name[1]))

            pe.wait_ge(s_wqk_l, 1)
            pe.wait_ge(s_pool_c, 3)
            attention(0, False)
            pe.wait_ge(s_shared, PARTS)
            with pe.Fori(1, B) as b:
                attention(b, True)

            u0 = 8 * (B - 1)
            def last_up(i, which):
                shared_up(u0 + i, 2 * (i % TB) + i // TB, which, False)

            def last_down(i):
                pe.wait_ge(s_yacc, TT - TB + i)
                down(u0 + i, i // TB * WC, i % 2, True, True).then_inc(s_y, 1)

            for t in range(TB):
                pe.wait_ge(s_xt_l, TT - TB + t + 1)
                for_c = [(c * P, c * UP + F) for c in range(KC)]
                o = product3(b_of["G"][:, t * E:(t + 1) * E],
                             [(xTs_h[:, t, x:x + P], xTs_l[:, t, x:x + P], ring_h[:, w:w + E], ring_l[:, w:w + E]) for x, w in for_c])
            o.then_inc(s_lg_ps, 1)

            last_up(0, 0)
            last_up(0, 1)
            pe.wait_ge(s_mask, 1)
            t_.matmul(b_rank[0][:, 0:TT * E], upper[:, :], mask[:, :], start=True, stop=True)
            t_.matmul(b_rank[1][:, 0:TT * E], ones[:, :], mask[:, :], start=True, stop=True).then_inc(s_rank_ps, 1)
            for i in range(1, 8):
                last_up(i, 0)
                turn_g(u0 + i - 1)
                last_up(i, 1)
                last_down(i - 1)

            def turn_x(k, landed):
                pe.wait_ge(s_xs[k], landed)
                for c in range(KC):
                    o = t_.transpose(b_xT[:, c * P:(c + 1) * P], xs[:, k, c * P:(c + 1) * P], ident[:, :])
                o.then_inc(s_xT_ps, 1)

            turn_x(0, 16)
            r = pe.value_load(tile_tab[0:1, IN_RING, 0:1], min_val=0, max_val=(RING - 1) * WC)
            w = pe.value_load(tile_tab[0:1, SPLIT, 0:1], min_val=3, max_val=3 * E)
            xh, xl = (x[:, :, :].rearrange("p c n -> p (c n)") for x in (xT_h, xT_l))
            pe.wait_ge(s_xT_l, 1)
            pe.wait_ge(s_silu, 2 * TT + 1)
            pe.wait_ge(s_wlo, w)
            up(0, r, xh, xl)
            turn_g(2 * TT - 1)
            up(1, r, xh, xl)
            turn_x(1, 16)
            last_down(7)
            pe.wait_ge(s_yacc, YACC)

            def routed(t, k, j, nxt, turn):
                if nxt:
                    r = pe.value_load(tile_tab[0:1, IN_RING, bass.ds(t + 1, 1)], min_val=0, max_val=(RING - 1) * WC)
                    w = pe.value_load(tile_tab[0:1, SPLIT, bass.ds(t + 1, 1)], min_val=3, max_val=3 * E)
                    pe.wait_ge(s_xT_l, t + 2)
                    pe.wait_ge(s_silu, t + (2 * TT + 2))
                    pe.wait_ge(s_wlo, w)
                    up(0, r, xh, xl)
                turn_g(t + 2 * TT)
                if nxt:
                    up(1, r, xh, xl)
                if turn:
                    turn_x(k, j * 16 + 32)
                r0 = pe.value_load(tile_tab[0:1, IN_RING, bass.ds(t, 1)], min_val=0, max_val=(RING - 1) * WC)
                pe.wait_ge(s_ycp, t + 1)
                down(t + 2 * TT, r0, k, True, True).then_inc(s_y, 1)

            with pe.Fori(0, LT // 4) as j:
                for k in range(4):
                    routed(j * 4 + k, k % 2, j * 2 + k // 2, True, True)
            n_used = pe.value_load(used[0:1, :], min_val=LT, max_val=RT)
            for t in range(LT, RT):
                with pe.If(n_used > t):
                    routed(t, t % 2, t // 2, t + 1 < RT, t + 2 < RT)


def kernel(**inputs):
    import numpy as np
    import concourse.bacc as bacc
    from concourse.bass_utils import run_bass_kernel_spmd as run

    a = {k: np.asarray(v) for k, v in inputs.items()}

    def expert(w1, w3, w2, router=None):
        if router is None:
            router = np.zeros((D, E), w1.dtype)
        up = np.concatenate([w1.reshape(KC, P, F), router.reshape(KC, P, E), w3.reshape(KC, P, F)], axis=2).transpose(1, 0, 2)
        pad = np.concatenate([w2, np.zeros((len(FCH) * P - F, D), w2.dtype)])
        return np.concatenate([up.reshape(P, W13), pad.reshape(len(FCH), P, D).transpose(1, 0, 2).reshape(P, W2C)], axis=1)

    sw1, sw3, sw2 = (a["L0_ffn_" + n].T for n in ("sw1", "sw3", "sw2"))
    parts = [expert(sw1[:, s:s + F], sw3[:, s:s + F], sw2[s:s + F], r) for s, r in ((0, a["L0_ffn_gate_w"].T), (F, None))]
    parts += [expert(a["L0_ffn_W1"][e], a["L0_ffn_W3"][e], a["L0_ffn_W2"][e]) for e in range(E)]
    arrays = {
        "x": a["x"],
        "ctxT": a["ctx_1024"].transpose(0, 2, 1),
        "wqk": np.concatenate([a["L0_xattn_Wq"], a["L0_xattn_Wk"]]).T,
        "bqk": np.stack([a["L0_xattn_bq"], a["L0_xattn_bk"]], axis=1),
        "rbias": np.broadcast_to(a["L0_ffn_router_bias"], (P, E)),
        "gates": np.broadcast_to(np.concatenate([a["g_xattn"], a["g_ffn"]]), (P, 2)),
        "wall": np.concatenate(parts, axis=1),
    }
    arrays = {k: np.ascontiguousarray(v) for k, v in arrays.items()}
    nc = bacc.Bacc("TRN2", target_bir_lowering=False, num_devices=1)
    args = [nc.dram_tensor(k, v.shape, mybir.dt.from_np(v.dtype), kind="ExternalInput").ap() for k, v in arrays.items()]
    args.append(nc.dram_tensor("out", (TT * P + P, D), F32, kind="ExternalOutput").ap())
    args.append(nc.dram_tensor("xn_dram", (TT * P, D), F32, kind="Internal").ap())
    args.append(nc.dram_tensor("xs_dram", (RT * P, XW), F32, kind="Internal").ap())
    flamingo_kernel(nc, *args)
    return run(nc, [arrays], core_ids=[0]).results[0]["out"][:TT * P].reshape(B, L, D)
```
